# Optimizing a Trainium2 kernel written in Bass

```python
import numpy as np
import jax
import jax.numpy as jnp

def _softmax(x, axis=-1):
    return jax.nn.softmax(x, axis=axis)

def _gelu(x):
    return jax.nn.gelu(x, approximate=True)

def _silu(x):
    return jax.nn.silu(x)

def _sigmoid(x):
    return jax.nn.sigmoid(x)

def _layernorm(x, axis=-1, eps=1e-05):
    m = jnp.mean(x, axis=axis, keepdims=True)
    v = jnp.var(x, axis=axis, keepdims=True)
    return (x - m) / jnp.sqrt(v + eps)

def _scatter_add(tgt, idx, src, axis=0):
    return tgt.at[idx].add(src)

def _segment_sum(src, seg, n):
    return jax.ops.segment_sum(src, seg, n)
kernel_name = 'mk_gnn_preln_d2_gnn_r64_d87d3c'

def setup_inputs(seed: int=0):
    np.random.seed(seed)
    _w = jnp.asarray

    def _rec_inputs():
        import jax
        import jax.numpy as jnp
        _gk = jax.random.key(seed)
        x = -0.0003713 + 1 * jax.random.normal(jax.random.fold_in(_gk, 1), (100000, 128), jnp.float32)
        src = jax.random.randint(jax.random.fold_in(_gk, 2), (25000,), 0, 100000, jnp.int32)
        dst = jnp.minimum((100000 * jax.random.uniform(jax.random.fold_in(_gk, 3), (25000,)) ** 2.0).astype(jnp.int32), 99999)
        _o = jnp.argsort(dst, stable=True)
        src = src[_o]
        dst = dst[_o]
        edge_attr_64 = 0.000189758 + 1.00013 * jax.random.normal(jax.random.fold_in(_gk, 13), (25000, 64), jnp.float32)
        return (x, src, dst, edge_attr_64)
    x, src, dst, edge_attr_64 = _rec_inputs()

    def _L0_gnn_setup():
        import jax, jax.numpy as jnp
        import numpy as np
        N_NODES = 100000
        N_EDGES = 12500
        F_IN = 128

        def _seg_mean(vals, idx, deg, n):
            s = jax.ops.segment_sum(vals, idx, num_segments=n)
            return s / jnp.maximum(deg, 1.0)[:, None]
        key = jax.random.key(seed)
        ks = jax.random.split(key, 8)
        feat = jax.random.normal(ks[0], (N_NODES, F_IN), dtype=jnp.float32)
        src = jax.random.randint(ks[1], (N_EDGES,), 0, N_NODES, dtype=jnp.int32)
        dst = jax.random.randint(ks[2], (N_EDGES,), 0, N_NODES, dtype=jnp.int32)
        scale1 = 1.0 / np.sqrt(3 * F_IN)
        W1 = jax.random.normal(ks[3], (3 * F_IN, F_IN), dtype=jnp.float32) * scale1
        b1 = jax.random.normal(ks[4], (F_IN,), dtype=jnp.float32) * scale1
        W2 = jax.random.normal(ks[5], (3 * F_IN, F_IN), dtype=jnp.float32) * scale1
        b2 = jax.random.normal(ks[6], (F_IN,), dtype=jnp.float32) * scale1
        return {'feat': feat, 'src': src, 'dst': dst, 'W1': W1, 'b1': b1, 'W2': W2, 'b2': b2}
    _L0_gnn_all = _L0_gnn_setup()
    _L0_gnn_in = {k: v for k, v in _L0_gnn_all.items() if k in ('W1', 'b1', 'W2', 'b2')}
    del _L0_gnn_all

    def _L1_gnn_setup():
        import jax, jax.numpy as jnp
        import numpy as np
        N_NODES = 50000
        N_EDGES = 12500
        N_GRAPHS = 64
        NEG_SLOPE = 0.01

        def leaky_relu(x):
            return jnp.where(x >= 0, x, NEG_SLOPE * x)
        key = jax.random.key(seed)
        ks = jax.random.split(key, 10)
        x = jax.random.normal(ks[0], (N_NODES, 128), dtype=jnp.float32)
        edge_index = jax.random.randint(ks[1], (2, N_EDGES), 0, N_NODES, dtype=jnp.int64)
        edge_attr = jax.random.normal(ks[2], (N_EDGES, 64), dtype=jnp.float32)
        u = jax.random.normal(ks[3], (N_GRAPHS, 64), dtype=jnp.float32)
        batch = jnp.sort(jax.random.randint(ks[4], (N_NODES,), 0, N_GRAPHS, dtype=jnp.int64))
        s1 = 1.0 / np.sqrt(256)
        w1 = jax.random.uniform(ks[5], (256, 256), jnp.float32, -s1, s1)
        b1 = jnp.zeros((256,), jnp.float32)
        w2 = jax.random.uniform(ks[6], (256, 256), jnp.float32, -s1, s1)
        b2 = jnp.zeros((256,), jnp.float32)
        w3 = jax.random.uniform(ks[7], (256, 128), jnp.float32, -s1, s1)
        b3 = jnp.zeros((128,), jnp.float32)
        return {'x': x, 'edge_index': edge_index, 'edge_attr': edge_attr, 'u': u, 'batch': batch, 'w1': w1, 'b1': b1, 'w2': w2, 'b2': b2, 'w3': w3, 'b3': b3}
    _L1_gnn_all = _L1_gnn_setup()
    _L1_gnn_in = {k: v for k, v in _L1_gnn_all.items() if k in ('u', 'w1', 'b1', 'w2', 'b2', 'w3', 'b3')}
    del _L1_gnn_all
    return {'x': x, 'src': src, 'dst': dst, 'edge_attr_64': edge_attr_64, 'L0_gnn_W1': _L0_gnn_in['W1'], 'L0_gnn_b1': _L0_gnn_in['b1'], 'L0_gnn_W2': _L0_gnn_in['W2'], 'L0_gnn_b2': _L0_gnn_in['b2'], 'L1_gnn_u': _L1_gnn_in['u'], 'L1_gnn_w1': _L1_gnn_in['w1'], 'L1_gnn_b1': _L1_gnn_in['b1'], 'L1_gnn_w2': _L1_gnn_in['w2'], 'L1_gnn_b2': _L1_gnn_in['b2'], 'L1_gnn_w3': _L1_gnn_in['w3'], 'L1_gnn_b3': _L1_gnn_in['b3']}

def reference(x, src, dst, edge_attr_64, L0_gnn_W1, L0_gnn_b1, L0_gnn_W2, L0_gnn_b2, L1_gnn_u, L1_gnn_w1, L1_gnn_b1, L1_gnn_w2, L1_gnn_b2, L1_gnn_w3, L1_gnn_b3):
    import jax
    import jax.numpy as jnp

    def _L0_gnn_ref(feat, src, dst, W1, b1, W2, b2):
        import jax, jax.numpy as jnp
        import numpy as np
        N_NODES = 100000
        N_EDGES = 12500
        F_IN = 128

        def _seg_mean(vals, idx, deg, n):
            s = jax.ops.segment_sum(vals, idx, num_segments=n)
            return s / jnp.maximum(deg, 1.0)[:, None]
        n = feat.shape[0]
        ones = jnp.ones((src.shape[0],), dtype=feat.dtype)
        deg_in = jax.ops.segment_sum(ones, dst, num_segments=n)
        deg_out = jax.ops.segment_sum(ones, src, num_segments=n)

        def layer(h, W, b, act):
            fwd_neigh = _seg_mean(h[src], dst, deg_in, n)
            bwd_neigh = _seg_mean(h[dst], src, deg_out, n)
            out = jnp.concatenate([h, fwd_neigh, bwd_neigh], axis=1) @ W + b
            return act(out)
        h = layer(feat, W1, b1, jax.nn.relu)
        h = layer(h, W2, b2, lambda x: x)
        return h

    def _L1_gnn_ref(x, edge_index, edge_attr, u, batch, w1, b1, w2, b2, w3, b3):
        import jax, jax.numpy as jnp
        import numpy as np
        N_NODES = 50000
        N_EDGES = 12500
        N_GRAPHS = 64
        NEG_SLOPE = 0.01

        def leaky_relu(x):
            return jnp.where(x >= 0, x, NEG_SLOPE * x)
        col = edge_index[1]
        agg = jax.ops.segment_sum(edge_attr, col, num_segments=x.shape[0])
        h = jnp.concatenate([x, agg, u[batch]], axis=1)
        h = leaky_relu(h @ w1 + b1)
        h = leaky_relu(h @ w2 + b2)
        return h @ w3 + b3
    edge_index = jnp.stack([src, dst])
    batch0 = jnp.zeros((100000,), jnp.int32)
    h = jnp.maximum(_layernorm(x, axis=-1), 0.0)
    x = x + _L0_gnn_ref(h, src, dst, L0_gnn_W1, L0_gnn_b1, L0_gnn_W2, L0_gnn_b2)
    h = jnp.maximum(_layernorm(x, axis=-1), 0.0)
    x = x + _L1_gnn_ref(h, edge_index, edge_attr_64, L1_gnn_u, batch0, L1_gnn_w1, L1_gnn_b1, L1_gnn_w2, L1_gnn_b2, L1_gnn_w3, L1_gnn_b3)
    return x

_drawn_inputs = setup_inputs


def setup_inputs(seed=0):
    import zlib

    import numpy as np

    out = dict(_drawn_inputs(seed))
    spreads = {'L1_gnn_b1': (0.0, 0.564), 'L1_gnn_b2': (0.0, 0.1), 'L1_gnn_b3': (0.0, 0.1)}
    factors = {'edge_attr_64': 2.998}
    for name, (base, spread) in spreads.items():
        noise = np.random.default_rng([zlib.crc32(name.encode()), seed]).standard_normal(out[name].shape)
        drawn = base * np.exp(spread * noise) if base else spread * noise
        out[name] = jnp.asarray(drawn.astype(out[name].dtype))
    for name, factor in factors.items():
        out[name] = (out[name] * factor).astype(out[name].dtype)
    return out
```

```python
from contextlib import ExitStack

import concourse.bass as bass
from concourse import mybir

ALU = mybir.AluOpType
ACT = mybir.ActivationFunctionType
F32 = mybir.dt.float32
BF16 = mybir.dt.bfloat16
F16 = mybir.dt.float16
I32 = mybir.dt.int32

P = 128
EPS = 1e-5
SLOPE = 0.01


def gnn_kernel(nc, x, src, dst, edge_attr, W1, b1, W2, b2, u, w1, b1m, w2, b2m, w3, b3, out):
    N, F = x.shape
    E, FA = edge_attr.shape
    H = w1.shape[1]
    HB = H // P
    ROW = F + FA
    T = 4
    BLK = T * P
    EG = 2 * P
    G = (E + EG - 1) // EG
    GS = 2 * EG
    STEPS = 2 * G
    assert F == P and (STEPS - 1) * BLK < N <= STEPS * BLK and STEPS % 4 == 0
    TAIL = E - (G - 1) * EG
    HI = STEPS * T
    NK = HI * P
    assert N + EG <= NK
    DUMP = NK
    NR = NK + GS
    HALF = HI // 2
    assert (NR - N) % 8 == 0 and (NR - N) // 8 <= P
    CH = 7
    CW = HI // CH
    assert CW * CH == HI and CW <= P and HALF <= 512

    pre1 = nc.dram_tensor("pre1", (NR, F), F32, kind="Internal").ap()
    node1 = nc.dram_tensor("node1", (NR, ROW), F32, kind="Internal").ap()
    msg1 = nc.dram_tensor("msg1", (G, P, 4, F), F32, kind="Internal").ap()
    msg2 = nc.dram_tensor("msg2", (G, P, 4, F), F32, kind="Internal").ap()
    keyrow = nc.dram_tensor("keyrow", (G, GS), F32, kind="Internal").ap()
    recip_in = nc.dram_tensor("recip_in", (NK, 1), F32, kind="Internal").ap()
    recip_out = nc.dram_tensor("recip_out", (NK, 1), F32, kind="Internal").ap()

    with ExitStack() as ctx:
        def sb(name, shape, dt=F32):
            return ctx.enter_context(nc.sbuf_tensor(name, shape, dt))

        def sem(name):
            return ctx.enter_context(nc.semaphore(name))

        bank = [ctx.enter_context(nc.psum_tensor(f"bank{i}", [P, 512], F32)) for i in range(8)]

        ident = sb("ident", [P, P])
        zeros = sb("zeros", [P, 8 * ROW])
        ones = sb("ones", [1, P])
        later = sb("later", [P, GS])
        iota_hi = sb("iota_hi", [P, HI], F16)
        iota_lo = sb("iota_lo", [P, P], F16)
        dumpcol = sb("dumpcol", [P, 4])
        dumpi = sb("dumpi", [P, 4], I32)
        W1s = sb("W1s", [P, 3, F])
        W2s = sb("W2s", [P, 3, F])
        b1s = sb("b1s", [1, F])
        b2s = sb("b2s", [1, F])
        w1x = sb("w1x", [P, H])
        w1a = sb("w1a", [FA, H])
        w1u = sb("w1u", [FA, H])
        u0 = sb("u0", [FA, 1])
        w2s = sb("w2s", [P, HB, H])
        w3s = sb("w3s", [P, HB, F])
        b3s = sb("b3s", [P, F])
        bias1 = sb("bias1", [P, HB])
        bias2 = sb("bias2", [P, HB])
        bias1_small = sb("bias1_small", [P, HB])
        bias2_small = sb("bias2_small", [P, HB])
        ids_int = sb("ids_int", [G, 2, EG], I32)
        ids = sb("ids", [G, GS])
        keys = sb("keys", [P, 2, 4, G])
        repkey = sb("repkey", [P, 4, G])
        keyi = sb("keyi", [P, 4 * G], I32)
        part = sb("part", [P, 2, 4 * G], I32)
        hilo = sb("hilo", [P, 2, 4, G])
        recip = sb("recip", [P, 4, G])
        recip_buf = sb("recip_buf", [P, 4, 2])
        eps = sb("eps", [P, 1])
        onehot_hi = sb("onehot_hi", [P, 4, HI], BF16)
        onehot_lo = sb("onehot_lo", [P, 4, P], BF16)
        degree = sb("degree", [P, 2, HI])
        degree_T = sb("degree_T", [CW, 2, CH, P])
        rows = sb("rows", [P, 4, 6, F])
        resid = sb("resid", [P, 4, T, F])
        normed = sb("normed", [P, 4, 6, F])
        stats = sb("stats", [P, 4, 6, 6])
        moments = sb("moments", [P, 4, 6, 2])
        spread = sb("spread", [P, 4, 6])
        rstd = sb("rstd", [P, 4, 6])
        index = sb("index", [P, 4, 4], I32)
        hT = sb("hT", [P, 4, 6, P])
        node_out = sb("node_out", [P, 4, T, ROW])
        edge_out = sb("edge_out", [P, 4, 2, F])
        group_msg = sb("group_msg", [P, 2, 4, ROW])
        keyall = sb("keyall", [P, 2, GS])
        same = sb("same", [P, 2, 4, GS])
        masked = sb("masked", [P, 4, GS])
        repeats = sb("repeats", [P, 2, 4])
        todump = sb("todump", [P, 2, 4])
        rep_index = sb("rep_index", [P, 2, 4], I32)
        summed = sb("summed", [P, 2, 4, ROW])
        aT = sb("aT", [FA, BLK])
        small1 = sb("small1", [P, HB, BLK])
        z1 = sb("z1", [P, HB, BLK])
        small2 = sb("small2", [P, HB, BLK])
        z2 = sb("z2", [P, HB, BLK])

        block = ctx.enter_context(nc.Block())

        s_w = sem("weights_loaded")
        s_bias = sem("mlp_biases_loaded")
        s_pool_const = sem("pool_constants")
        s_pads = sem("ids_pads_written")
        s_ids = sem("ids_loaded")
        s_tails = sem("tail_rows_zeroed")
        s_idsf = sem("ids_as_floats")
        s_keyrow = sem("keyrow_stored")
        s_keysT = sem("keys_transposed")
        s_keys = sem("keys_ready")
        s_vprep = sem("vector_prelude_steps")
        s_onehot = sem("onehots_written")
        s_count = sem("onehots_counted")
        s_deg = sem("degrees_ready")
        s_degT = sem("degrees_transposed")
        s_degc = sem("degrees_copied")
        s_recip = sem("recip_tables_stored")
        s_ub = sem("u_product_ready")
        s_b1c = sem("bias_columns_ready")
        s_zcol = sem("attribute_columns_zeroed")
        s_kept = sem("recips_kept")

        class Dense:
            def __init__(self, n):
                self.load = [sem(f"{n}_rows_loaded{b}") for b in range(4)]
                self.index = sem(f"{n}_index_ready")
                self.gather = [sem(f"{n}_rows_gathered{b}") for b in range(4)]
                self.recip = [sem(f"{n}_recip_gathered{b}") for b in range(4)]
                self.stats = sem(f"{n}_stats")
                self.moments = sem(f"{n}_moments")
                self.spread = sem(f"{n}_spread")
                self.rstd = sem(f"{n}_rstd")
                self.normed = sem(f"{n}_normed")
                self.T = sem(f"{n}_transposed")
                self.hT = sem(f"{n}_hT_copied")
                self.mm = sem(f"{n}_products")
                self.edge = sem(f"{n}_edge_out_copied")
                self.node = sem(f"{n}_node_out_copied")
                self.store_node = [sem(f"{n}_node_stored{b}") for b in range(4)]
                self.store_edge = [sem(f"{n}_edge_stored{b}") for b in range(4)]

        class Scatter:
            def __init__(self, n):
                self.msg = [sem(f"{n}_messages_loaded{b}") for b in range(2)]
                self.keyall = [sem(f"{n}_keys_loaded{b}") for b in range(2)]
                self.same = sem(f"{n}_same_written")
                self.repeats = sem(f"{n}_repeats_counted")
                self.todump = sem(f"{n}_way_to_dump")
                self.moved = sem(f"{n}_offset_chosen")
                self.index = sem(f"{n}_index_ready")
                self.mm = sem(f"{n}_summed_product")
                self.copied = sem(f"{n}_sums_copied")
                self.done = [sem(f"{n}_added{b}") for b in range(2)]

        passed = {nc.vector.engine: sem("vector_waits_passed"), nc.gpsimd.engine: sem("pool_waits_passed")}
        A, C = Dense("a"), Dense("c")
        B, D = Scatter("b"), Scatter("d")
        e_load = [sem(f"e_rows_loaded{b}") for b in range(4)]
        e_store = [sem(f"e_out_stored{b}") for b in range(4)]
        e_stats, e_moments, e_spread = sem("e_stats"), sem("e_moments"), sem("e_spread")
        e_rstd, e_normed, e_resid = sem("e_rstd"), sem("e_normed"), sem("e_resid_biased")
        e_T, e_hT = sem("e_transposed"), sem("e_hT_copied")
        e_L1, e_small1, e_z1 = sem("e_L1"), sem("e_small1"), sem("e_z1")
        e_L2, e_small2, e_z2 = sem("e_L2"), sem("e_small2"), sem("e_z2")
        e_L3, e_out = sem("e_L3"), sem("e_out")

        def sweep(eng, n, step):
            step(0)
            with eng.Fori(1, n - 1) as j:
                step(j)
            step(n - 1)

        class Step:

            def __init__(self, q, r):
                q, self.b = q + r // 4, r % 4
                self.k, self.turn, self.g, self.half = q * 4 + self.b, q + 1, q * 2 + self.b // 2, self.b % 2
                self.known = isinstance(q, int)
                self.exists = not self.known or 0 <= self.k < STEPS
                self.last = self.known and self.k == STEPS - 1

            def after(self, n):
                return not self.known or self.k >= n

        def ticks(eng, tick, lag):
            for t in range(8):
                tick(lambda n, t=t: Step(0, t - n))
            with eng.Fori(2, STEPS // 4 - 1) as q:
                for t in range(4):
                    tick(lambda n, t=t: Step(q, t - n))
            for t in range(4 + lag):
                tick(lambda n, t=t: Step(STEPS // 4 - 1, t - n))

        def hold(eng):
            eng.sem_inc(passed[eng.engine], 1)

        def before(g, n):
            return not isinstance(g, int) or g >= n

        def block_of(table, st):
            base = N - BLK if st.last else st.k * BLK
            return table[bass.ds(base, BLK), :].rearrange("(p t) f -> p t f", t=T)

        @block.sync
        def _(sp):
            for dst_ap, src_ap in ((W1s[:], W1.rearrange("(c p) f -> p c f", p=P)),
                                   (W2s[:], W2.rearrange("(c p) f -> p c f", p=P)),
                                   (b1s[:], b1.rearrange("(a f) -> a f", a=1)),
                                   (b2s[:], b2.rearrange("(a f) -> a f", a=1)),
                                   (w1x[:], w1[0:F, :]), (w1a[:], w1[F:ROW, :]), (w1u[:], w1[ROW:ROW + FA, :]),
                                   (u0[:], u[0:1, :].rearrange("a f -> f a")),
                                   (w2s[:], w2.rearrange("(c p) f -> p c f", p=P)),
                                   (w3s[:], w3.rearrange("(c p) f -> p c f", p=P)),
                                   (b3s[:], b3.rearrange("(a f) -> a f", a=1).to_broadcast([P, F]))):
                sp.dma_start(dst_ap, src_ap).then_inc(s_w, 16)
            sp.wait_ge(s_pads, 1)
            for c, ends in enumerate((dst, src)):
                sp.dma_start(ids_int[0:G - 1, c, :],
                             ends[0:(G - 1) * EG].rearrange("(g e) -> g e", e=EG)).then_inc(s_ids, 16)
                sp.dma_start(ids_int[G - 1:G, c, 0:TAIL],
                             ends[(G - 1) * EG:E].rearrange("(g e) -> g e", g=1)).then_inc(s_ids, 16)
            for c, (col, vec) in enumerate(((bias1, b1m), (bias2, b2m))):
                sp.dma_start(col[:], vec.rearrange("(m p) -> p m", p=P), allow_slow_non_contiguous=True).then_inc(s_bias, 16)
            sp.wait_ge(s_pool_const, 1)
            for table, width in ((pre1, F), (node1, ROW)):
                sp.dma_start(table[N:NR, :].rearrange("(p r) f -> p (r f)", r=8), zeros[0:(NR - N) // 8, 0:8 * width])\
                    .then_inc(s_tails, 16)
            sp.wait_ge(s_idsf, 1)
            sp.dma_start(keyrow, ids[:]).then_inc(s_keyrow, 16)
            for c, table in enumerate((recip_in, recip_out)):
                sp.wait_ge(s_degc, c + 1)
                sp.dma_start(table.rearrange("(q r) a -> q (r a)", q=CW),
                             degree_T[:, c].rearrange("p c f -> p (c f)")).then_inc(s_recip, 16)

            def dense(S, source, with_x, target, width, msg):
                def tick(at):
                    st = at(0)
                    if st.exists:
                        if st.after(4):
                            sp.wait_ge(S.T if with_x else S.normed, st.k - 3)
                            if with_x:
                                sp.wait_ge(S.node, st.k - 3)
                        sp.dma_start(rows[:, st.b, 0:T, :], block_of(source, st)).then_inc(S.load[st.b], 16)
                        if with_x:
                            sp.dma_start(resid[:, st.b], block_of(x, st)).then_inc(S.load[st.b], 16)
                    st = at(3)
                    if st.exists:
                        sp.wait_ge(S.node, st.k + 1)
                        if st.last:
                            sp.wait_ge(S.store_node[st.b - 1], 16 * st.turn)
                        sp.dma_start(block_of(target, st), node_out[:, st.b, :, 0:width]).then_inc(S.store_node[st.b], 16)
                        sp.wait_ge(S.edge, st.k + 1)
                        sp.dma_start(msg[bass.ds(st.g, 1), :, st.half::2, :].rearrange("g p s f -> (g p) s f"),
                                     edge_out[:, st.b]).then_inc(S.store_edge[st.b], 16)
                ticks(sp, tick, 3)

            def scatter(S, X, msg, with_attr):
                if not with_attr:
                    sp.wait_ge(s_keyrow, 16)
                for b in range(4):
                    sp.wait_ge(X.store_edge[b], 16 * STEPS // 4)

                def step(g, b, uses):
                    if before(g, 2):
                        sp.wait_ge(S.mm, g - 1)
                    one = msg[bass.ds(g, 1)].rearrange("g p s f -> (g p) s f")
                    sp.dma_start(group_msg[:, b, :, 0:F], one).then_inc(S.msg[b], 16)
                    if with_attr:
                        if isinstance(g, int) and g == G - 1:
                            sp.dma_start(group_msg[:, b, 0, F:ROW], edge_attr[g * EG:g * EG + P, :]).then_inc(S.msg[b], 16)
                            sp.dma_start(group_msg[0:TAIL - P, b, 1, F:ROW], edge_attr[g * EG + P:E, :]).then_inc(S.msg[b], 16)
                        else:
                            for s in range(2):
                                sp.dma_start(group_msg[:, b, s, F:ROW], edge_attr[bass.ds(g * EG + s * P, P), :])\
                                    .then_inc(S.msg[b], 16)
                    sp.dma_start(keyall[:, b, :], keyrow[bass.ds(g, 1), :].to_broadcast([P, GS])).then_inc(S.keyall[b], 16)

                sweep(sp, G // 2, lambda j: [step(j * 2 + b, b, j + 1) for b in range(2)])

            dense(A, x, False, pre1, F, msg1)
            scatter(B, A, msg1, False)
            for b in range(2):
                sp.wait_ge(B.done[b], 64 * G // 2)
            dense(C, pre1, True, node1, ROW, msg2)
            scatter(D, C, msg2, True)
            for b in range(2):
                sp.wait_ge(D.done[b], 64 * G // 2)

            def tick(at):
                st = at(0)
                if st.exists:
                    if st.after(4):
                        sp.wait_ge(e_T, st.k - 3)
                        sp.wait_ge(e_resid, st.k - 3)
                    sp.dma_start(node_out[:, st.b], block_of(node1, st)).then_inc(e_load[st.b], 16)
                st = at(3)
                if st.exists:
                    sp.wait_ge(e_out, st.k + 1)
                    if st.last:
                        sp.wait_ge(e_store[st.b - 1], 16 * st.turn)
                    sp.dma_start(block_of(out, st), rows[:, st.b, 0:T, :]).then_inc(e_store[st.b], 16)
            ticks(sp, tick, 3)
            for b in range(4):
                sp.wait_ge(e_store[b], 16 * STEPS // 4)

        @block.gpsimd
        def _(pool):
            pool.memset(zeros[:], 0.0).then_inc(s_pool_const, 1)
            pool.iota(ids_int[:], pattern=[[0, 2], [1, EG]], base=N, channel_multiplier=0).then_inc(s_pads, 1)
            pool.memset(ident[:], 0.0).then_inc(s_pool_const, 1)
            pool.memset(ones[:], 1.0).then_inc(s_pool_const, 1)
            pool.memset(later[:], 1.0).then_inc(s_pool_const, 1)
            pool.iota(iota_hi[:], pattern=[[1, HI]], base=0, channel_multiplier=0,
                      allow_small_or_imprecise_dtypes=True).then_inc(s_pool_const, 1)
            pool.iota(iota_lo[:], pattern=[[1, P]], base=0, channel_multiplier=0,
                      allow_small_or_imprecise_dtypes=True).then_inc(s_pool_const, 1)
            pool.iota(dumpi[:], pattern=[[P, 4]], base=DUMP, channel_multiplier=1).then_inc(s_pool_const, 1)
            pool.wait_ge(s_pool_const, 7)
            pool.affine_select(out=ident[:], in_=ident[:], compare_op=ALU.not_equal, fill=1.0, base=0,
                               pattern=[[-1, P]], channel_multiplier=1).then_inc(s_pool_const, 1)
            pool.affine_select(out=later[:], in_=later[:], compare_op=ALU.is_gt, fill=0.0, base=0,
                               pattern=[[1, GS]], channel_multiplier=-1).then_inc(s_pool_const, 1)
            pool.tensor_copy(dumpcol[:], dumpi[:]).then_inc(s_pool_const, 1)
            pool.memset(node_out[:], 0.0).then_inc(s_zcol, 1)

            def dense(S, table, with_recip):
                def tick(at):
                    st = at(0)
                    b = st.b
                    if st.after(4):
                        pool.wait_ge(S.normed if with_recip else S.T, st.k - 3)
                    pool.wait_ge(S.index, st.k + 1)
                    hold(pool)
                    for slot, col in ((T, 1), (T + 1, 0)):
                        pool.indirect_dma_start(rows[:, b, slot, :], None, table,
                                                bass.IndirectOffsetOnAxis(ap=index[:, b, col:col + 1], axis=0))\
                            .then_inc(S.gather[b], 16)
                    if with_recip:
                        if st.after(4):
                            pool.wait_ge(s_kept, st.k - 3)
                        hold(pool)
                        for slot, tab in enumerate((recip_in, recip_out)):
                            pool.indirect_dma_start(recip_buf[:, b, slot:slot + 1], None, tab,
                                                    bass.IndirectOffsetOnAxis(ap=index[:, b, 2 + slot:3 + slot], axis=0))\
                                .then_inc(S.recip[b], 16)
                ticks(pool, tick, 0)

            def scatter(S, X, target, width):
                for b in range(4):
                    pool.wait_ge(X.store_node[b], 16 * STEPS // 4)
                pool.wait_ge(s_tails, 32)

                def step(g, b, uses):
                    pool.wait_ge(S.copied, g + 1)
                    pool.wait_ge(S.index, g + 1)
                    if before(g, 1):
                        last = (uses - 1) if b == 0 else uses
                        pool.wait_ge(S.done[1 - b], last * 64)
                    hold(pool)
                    for s in range(4):
                        pool.indirect_dma_start(target, bass.IndirectOffsetOnAxis(ap=rep_index[:, b, s:s + 1], axis=0),
                                                summed[:, b, s, 0:width], None, compute_op=ALU.add).then_inc(S.done[b], 16)

                sweep(pool, G // 2, lambda j: [step(j * 2 + b, b, j + 1) for b in range(2)])

            pool.wait_ge(s_recip, 32)
            dense(A, x, True)
            scatter(B, A, pre1, F)
            for b in range(2):
                pool.wait_ge(B.done[b], 64 * G // 2)
            dense(C, pre1, False)
            scatter(D, C, node1, ROW)

            def tick(at):
                st = at(0)
                b = st.b
                pool.wait_ge(e_load[b], 16 * st.turn)
                if st.after(4):
                    pool.wait_ge(e_out, st.k - 3)
                for s in range(T):
                    last = pool.tensor_tensor(resid[:, b, s, :], node_out[:, b, s, 0:F], b3s[:], ALU.add)
                last.then_inc(e_resid, 1)
            ticks(pool, tick, 0)

        @block.scalar
        def _(act):
            act.wait_ge(s_keys, 1)

            def stage_index(S, st):
                if st.after(4):
                    act.wait_ge(S.gather[st.b], 32 * (st.turn - 1))
                    if S is A:
                        act.wait_ge(S.recip[st.b], 32 * (st.turn - 1))
                act.activation(index[:, st.b, :].rearrange("p (a s) -> p a s", a=2),
                               keys[:, :, st.half::2, bass.ds(st.g, 1)].rearrange("p a s g -> p a (s g)"),
                               ACT.Copy).then_inc(S.index, 1)

            def copy_hT(S, st):
                act.wait_ge(S.T, st.k + 1)
                o = 2 * (st.b % 2)
                act.activation(hT[:, st.b, 0:4, :].rearrange("p s f -> p (s f)"), bank[o][:], ACT.Relu)
                act.activation(hT[:, st.b, 4:6, :].rearrange("p s f -> p (s f)"), bank[o + 1][:, 0:2 * P], ACT.Relu)\
                    .then_inc(S.hT, 1)

            def copy_edge(S, st, scale):
                if st.after(4):
                    act.wait_ge(S.store_edge[st.b], 16 * (st.turn - 1))
                for s in range(2):
                    last = act.activation(edge_out[:, st.b, s, :], bank[5 + 2 * (st.b % 2)][:, s * P:(s + 1) * P],
                                          ACT.Copy, scale=scale(s))
                last.then_inc(S.edge, 1)

            act.wait_ge(s_zcol, 2)
            for k in range(2):
                stage_index(A, Step(0, k))

            def tick(at):
                st = at(-2)
                if st.exists:
                    stage_index(A, st)
                st = at(0)
                if st.exists:
                    act.wait_ge(A.moments, st.k + 1)
                    act.activation(spread[:, st.b, :], moments[:, st.b, :, 1], ACT.Sqrt, bias=eps[:, 0:1]).then_inc(A.spread, 1)
                st = at(1)
                if st.exists:
                    copy_hT(A, st)
                st = at(2)
                if st.exists:
                    act.wait_ge(A.mm, st.k + 1)
                    if st.after(4):
                        act.wait_ge(A.store_node[st.b], 16 * (st.turn - 1))
                    act.activation(node_out[:, st.b, :, 0:F], bank[4 + 2 * (st.b % 2)][:].rearrange("p (t f) -> p t f", t=T),
                                   ACT.Copy).then_inc(A.node, 1)
                    act.wait_ge(A.recip[st.b], 32 * st.turn)
                    copy_edge(A, st, lambda s: recip_buf[:, st.b, s:s + 1])
                    act.activation(recip[:, st.half::2, bass.ds(st.g, 1)].rearrange("p s g -> p (s g)"),
                                   recip_buf[:, st.b, :], ACT.Copy).then_inc(s_kept, 1)
            ticks(act, tick, 2)

            def scatter(S, width):
                def step(g, b, uses):
                    act.wait_ge(S.mm, g + 1)
                    if before(g, 2):
                        act.wait_ge(S.done[b], 64 * (uses - 1))
                    if S is D:
                        act.activation(rep_index[:, b, :], repkey[:, :, bass.ds(g, 1)].rearrange("p s g -> p (s g)"),
                                       ACT.Copy).then_inc(S.index, 1)
                    for c in range(2):
                        last = act.activation(summed[:, b, 2 * c:2 * c + 2, 0:width],
                                              bank[4 + 2 * b + c][:].rearrange("p (s f) -> p s f", s=2)[:, :, 0:width],
                                              ACT.Copy)
                    last.then_inc(S.copied, 1)
                sweep(act, G // 2, lambda j: [step(j * 2 + b, b, j + 1) for b in range(2)])

            scatter(B, F)

            for k in range(2):
                stage_index(C, Step(0, k))

            def tick(at):
                st = at(-2)
                if st.exists:
                    stage_index(C, st)
                st = at(1)
                if st.exists:
                    copy_hT(C, st)
                st = at(2)
                if st.exists:
                    act.wait_ge(C.mm, st.k + 1)
                    copy_edge(C, st, lambda s: recip[:, st.half + 2 * s, bass.ds(st.g, 1)])
            act.wait_ge(s_kept, STEPS)
            ticks(act, tick, 2)
            scatter(D, ROW)

            act.wait_ge(s_b1c, 4)

            def scaled(st, products, first_bank, bias_small, small, ready):
                for m in range(HB):
                    act.wait_ge(products, st.k * HB + (m + 1))
                    act.activation(small[:, m, :], bank[first_bank + m][:], ACT.Identity, scale=SLOPE,
                                   bias=bias_small[:, m:m + 1]).then_inc(ready, 1)

            def tick(at):
                st = at(2)
                if st.exists:
                    scaled(st, e_L1, 0, bias1_small, small1, e_small1)
                st = at(0)
                if st.exists:
                    act.wait_ge(e_moments, st.k + 1)
                    act.activation(spread[:, st.b, 0:T], moments[:, st.b, 0:T, 1], ACT.Sqrt, bias=eps[:, 0:1])\
                        .then_inc(e_spread, 1)
                st = at(2)
                if st.exists:
                    scaled(st, e_L2, 2, bias2_small, small2, e_small2)
                st = at(1)
                if st.exists:
                    act.wait_ge(e_T, st.k + 1)
                    act.activation(hT[:, 0, 0:4, :].rearrange("p s f -> p (s f)"), bank[5][:], ACT.Relu)
                    act.activation(aT[:], bank[6][0:FA, :], ACT.Copy).then_inc(e_hT, 1)
            ticks(act, tick, 2)

        @block.vector
        def _(dve):
            dve.memset(eps[:], EPS).then_inc(s_zcol, 1)
            dve.wait_ge(s_ids, 64)
            dve.tensor_copy(ids[:], ids_int[:].rearrange("g c e -> g (c e)")).then_inc(s_idsf, 1)
            kk = keys[:, 1].rearrange("p s g -> p (s g)")
            dve.wait_ge(s_keysT, 1)
            dve.tensor_copy(kk, bank[0][:, 0:4 * G]).then_inc(s_vprep, 1)
            dve.wait_ge(s_vprep, 1)
            dve.tensor_scalar(keys[:, 0].rearrange("p s g -> p (s g)"), kk, float(N - 1), None, ALU.min).then_inc(s_keys, 1)
            dve.tensor_copy(keyi[:], kk).then_inc(s_vprep, 1)
            dve.wait_ge(s_vprep, 2)
            dve.tensor_scalar(part[:, 0], keyi[:], 7, None, ALU.logical_shift_right).then_inc(s_vprep, 1)
            dve.tensor_scalar(part[:, 1], keyi[:], P - 1, None, ALU.bitwise_and).then_inc(s_vprep, 1)
            dve.wait_ge(s_vprep, 4)
            dve.tensor_copy(hilo[:].rearrange("p a s g -> p a (s g)"), part[:]).then_inc(s_vprep, 1)
            dve.wait_ge(s_vprep, 5)
            dve.wait_ge(s_pool_const, 10)

            def onehots(g):
                for s in range(4):
                    if before(g, 1):
                        dve.wait_ge(s_count, g * 4 + s - 3)
                    dve.tensor_scalar(onehot_lo[:, s, :], iota_lo[:], hilo[:, 1, s, bass.ds(g, 1)], None, ALU.is_equal)
                    dve.tensor_scalar(onehot_hi[:, s, :], iota_hi[:], hilo[:, 0, s, bass.ds(g, 1)], None, ALU.is_equal)\
                        .then_inc(s_onehot, 1)
            sweep(dve, G, onehots)
            dve.wait_ge(s_count, 4 * G)
            for c in range(2):
                for h in range(2):
                    last = dve.tensor_scalar(degree[:, c, h * HALF:(h + 1) * HALF], bank[2 * c + h][:, 0:HALF], 1.0, None, ALU.max)
            last.then_inc(s_vprep, 1)
            dve.wait_ge(s_vprep, 6)
            dve.reciprocal(degree[:], degree[:]).then_inc(s_deg, 1)
            for c in range(2):
                dve.wait_ge(s_degT, c + 1)
                dve.tensor_copy(degree_T[:, c, 0:4, :], bank[4 + 2 * c][0:CW, :].rearrange("p (c f) -> p c f", f=P))
                dve.tensor_copy(degree_T[:, c, 4:CH, :], bank[5 + 2 * c][0:CW, 0:(CH - 4) * P].rearrange("p (c f) -> p c f", f=P))\
                    .then_inc(s_degc, 1)
            dve.wait_ge(s_ub, 1)
            dve.wait_ge(s_bias, 32)
            dve.tensor_tensor(bias1[:], bank[0][:, 0:HB], bias1[:], ALU.add).then_inc(s_b1c, 1)
            dve.wait_ge(s_b1c, 1)
            dve.tensor_scalar(bias1_small[:], bias1[:], SLOPE, None, ALU.mult).then_inc(s_b1c, 1)
            dve.tensor_scalar(bias2_small[:], bias2[:], SLOPE, None, ALU.mult).then_inc(s_b1c, 2)

            def moments_of(sems, st, n, source):
                s_stats, s_moments = sems
                for s in range(n):
                    last = dve.bn_stats(stats[:, st.b, s, :], source(st.b, s))
                last.then_inc(s_stats, 1)
                dve.wait_ge(s_stats, st.k + 1)
                hold(dve)
                for s in range(n):
                    last = dve.bn_aggr(moments[:, st.b, s, :], stats[:, st.b, s, :])
                last.then_inc(s_moments, 1)

            def normalise(sems, st, n, source):
                s_spread, s_rstd, s_normed, s_read = sems
                dve.wait_ge(s_spread, st.k + 1)
                dve.reciprocal(rstd[:, st.b, 0:n], spread[:, st.b, 0:n]).then_inc(s_rstd, 1)
                if st.after(4):
                    dve.wait_ge(s_read, st.k - 3)
                dve.wait_ge(s_rstd, st.k + 1)
                for s in range(n):
                    last = dve.tensor_scalar(normed[:, st.b, s, :], source(st.b, s), moments[:, st.b, s, 0:1],
                                             rstd[:, st.b, s:s + 1], ALU.subtract, ALU.mult)
                last.then_inc(s_normed, 1)

            def tick(at):
                st = at(0)
                if st.exists:
                    dve.wait_ge(A.load[st.b], 16 * st.turn)
                    dve.wait_ge(A.gather[st.b], 32 * st.turn)
                    moments_of((A.stats, A.moments), st, 6, lambda b, s: rows[:, b, s, :])
                st = at(1)
                if st.exists:
                    normalise((A.spread, A.rstd, A.normed, A.T), st, 6, lambda b, s: rows[:, b, s, :])
            ticks(dve, tick, 1)

            def scatter(S):
                def step(g, b, uses):
                    dve.wait_ge(S.keyall[b], 16 * uses)
                    if before(g, 2):
                        dve.wait_ge(S.mm, g - 1)
                    for s in range(4):
                        last = dve.tensor_scalar(same[:, b, s, s * P:GS], keyall[:, b, s * P:GS],
                                                 keys[:, 1, s, bass.ds(g, 1)], None, ALU.is_equal)
                    last.then_inc(S.same, 1)
                    if S is D:
                        return
                    dve.wait_ge(S.same, g + 1)
                    for s in range(4):
                        last = dve.tensor_tensor_reduce(masked[:, s, s * P:GS], same[:, b, s, s * P:GS], later[:, 0:GS - s * P],
                                                        1.0, 0.0, ALU.mult, ALU.add, repeats[:, b, s:s + 1])
                    dve.tensor_tensor(todump[:, b, :], dumpcol[:], keys[:, 1, :, bass.ds(g, 1)].rearrange("p s g -> p (s g)"),
                                      ALU.subtract).then_inc(S.todump, 1)
                    dve.wait_ge(S.todump, g + 1)
                    dve.scalar_tensor_tensor(out=todump[:, b, :], in0=repeats[:, b, :], scalar=0.0, in1=todump[:, b, :],
                                             op0=ALU.is_gt, op1=ALU.mult).then_inc(S.moved, 1)
                    dve.wait_ge(S.moved, g + 1)
                    rk = repkey[:, :, bass.ds(g, 1)].rearrange("p s g -> p (s g)")
                    dve.tensor_tensor(rk, keys[:, 1, :, bass.ds(g, 1)].rearrange("p s g -> p (s g)"), todump[:, b, :], ALU.add)\
                        .then_inc(S.repeats, 1)
                    if before(g, 2):
                        dve.wait_ge(S.done[b], 64 * (uses - 1))
                    dve.wait_ge(S.repeats, g + 1)
                    dve.tensor_scalar(rep_index[:, b, :], rk, 0.0, None, ALU.add).then_inc(S.index, 1)
                sweep(dve, G // 2, lambda j: [step(j * 2 + b, b, j + 1) for b in range(2)])
            scatter(B)

            def tick(at):
                st = at(2)
                if st.exists:
                    dve.wait_ge(C.mm, st.k + 1)
                    dve.wait_ge(C.load[st.b], 32 * st.turn)
                    if st.after(4):
                        dve.wait_ge(C.store_node[st.b], 16 * (st.turn - 1))
                    dve.tensor_tensor(node_out[:, st.b, :, 0:F], bank[4 + 2 * (st.b % 2)][:].rearrange("p (t f) -> p t f", t=T),
                                      resid[:, st.b], ALU.add).then_inc(C.node, 1)
            ticks(dve, tick, 2)
            scatter(D)

            def leaky(st, small_ready, first_bank, bias, small, z, ready):
                for m in range(HB):
                    dve.wait_ge(small_ready, st.k * HB + (m + 1))
                    dve.scalar_tensor_tensor(out=z[:, m, :], in0=bank[first_bank + m][:], scalar=bias[:, m:m + 1],
                                             in1=small[:, m, :], op0=ALU.add, op1=ALU.max).then_inc(ready, 1)

            def tick(at):
                st = at(2)
                if st.exists:
                    leaky(st, e_small1, 0, bias1, small1, z1, e_z1)
                st = at(1)
                if st.exists:
                    normalise((e_spread, e_rstd, e_normed, e_T), st, T, lambda b, s: node_out[:, b, s, 0:F])
                st = at(0)
                if st.exists:
                    dve.wait_ge(e_load[st.b], 16 * st.turn)
                    moments_of((e_stats, e_moments), st, T, lambda b, s: node_out[:, b, s, 0:F])
                st = at(3)
                if st.exists:
                    dve.wait_ge(e_L3, st.k + 1)
                    dve.wait_ge(e_resid, st.k + 1)
                    if st.after(4):
                        dve.wait_ge(e_store[st.b], 16 * (st.turn - 1))
                    dve.tensor_tensor(rows[:, st.b, 0:T, :], bank[4][:].rearrange("p (t f) -> p t f", t=T),
                                      resid[:, st.b], ALU.add).then_inc(e_out, 1)
                st = at(2)
                if st.exists:
                    leaky(st, e_small2, 2, bias2, small2, z2, e_z2)
            ticks(dve, tick, 3)

        @block.tensor
        def _(pe):
            pe.wait_ge(s_pool_const, 10)
            pe.wait_ge(s_idsf, 1)
            for s in range(4):
                last = pe.transpose(bank[0][:, s * G:(s + 1) * G], ids[:, s * P:(s + 1) * P], ident[0:G, 0:G])
            last.then_inc(s_keysT, 1)
            pe.wait_ge(s_keys, 1)

            def count(g):
                for s in range(4):
                    pe.wait_ge(s_onehot, g * 4 + s + 1)
                    for h in range(2):
                        last = pe.matmul(bank[2 * (s // 2) + h][:, 0:HALF], onehot_lo[:, s, :],
                                         onehot_hi[:, s, h * HALF:(h + 1) * HALF],
                                         start=(isinstance(g, int) and g == 0 and s % 2 == 0),
                                         stop=(isinstance(g, int) and g == G - 1 and s % 2 == 1))
                    last.then_inc(s_count, 1)
            sweep(pe, G, count)
            pe.wait_ge(s_deg, 1)
            for c in range(2):
                cols = degree[:, c].rearrange("p (q r) -> p r q", r=CH)
                for r in range(CH):
                    last = pe.transpose(bank[4 + 2 * c + r // 4][0:CW, (r % 4) * P:(r % 4 + 1) * P], cols[:, r, :], ident[:])
                last.then_inc(s_degT, 1)
            pe.wait_ge(s_w, 16 * 11)
            for m in range(HB):
                last = pe.matmul(bank[0][:, m:m + 1], w1u[:, m * P:(m + 1) * P], u0[:], start=True, stop=True)
            last.then_inc(s_ub, 1)

            def dense(S, W, b, source, ready):
                def tick(at):
                    st = at(1)
                    if st.exists:
                        ready(st)
                        if st.after(2):
                            pe.wait_ge(S.hT, st.k - 1)
                        for s in range(6):
                            last = pe.transpose(bank[s // 4 + 2 * (st.b % 2)][:, (s % 4) * P:(s % 4 + 1) * P],
                                                source[:, st.b, s, :], ident[:])
                        last.then_inc(S.T, 1)
                    st = at(2)
                    if st.exists:
                        pe.wait_ge(S.hT, st.k + 1)
                        if st.after(2):
                            pe.wait_ge(S.node, st.k - 1)
                            pe.wait_ge(S.edge, st.k - 1)
                        for s in range(T):
                            o = bank[4 + 2 * (st.b % 2)][:, s * P:(s + 1) * P]
                            pe.matmul(o, hT[:, st.b, s, :], W[:, 0, :], start=True, stop=False)
                            pe.matmul(o, ones[:], b[:], start=False, stop=True)
                        for s in range(2):
                            last = pe.matmul(bank[5 + 2 * (st.b % 2)][:, s * P:(s + 1) * P], hT[:, st.b, T + s, :],
                                             W[:, 1 + s, :], start=True, stop=True)
                        last.then_inc(S.mm, 1)
                ticks(pe, tick, 2)

            def scatter(S, with_attr):
                def step(g, b, uses):
                    pe.wait_ge(S.same, g + 1)
                    pe.wait_ge(S.msg[b], (48 if with_attr else 16) * uses)
                    if before(g, 2):
                        pe.wait_ge(S.copied, g - 1)
                    for i in range(4):
                        for j in range(i + 1):
                            w = ROW if with_attr and j < 2 else F
                            o = bank[4 + 2 * b + i // 2][:, (i % 2) * 256:(i % 2) * 256 + w]
                            last = pe.matmul(o, same[:, b, j, i * P:(i + 1) * P], group_msg[:, b, j, 0:w],
                                             start=(j == 0), stop=(j == i))
                    last.then_inc(S.mm, 1)
                sweep(pe, G // 2, lambda j: [step(j * 2 + b, b, j + 1) for b in range(2)])

            pe.wait_ge(s_degc, 2)
            pe.wait_ge(s_b1c, 1)
            dense(A, W1s, b1s, normed, lambda st: pe.wait_ge(A.normed, st.k + 1))
            pe.wait_ge(A.edge, STEPS)
            scatter(B, False)

            def c_ready(st):
                pe.wait_ge(C.load[st.b], 32 * st.turn)
                pe.wait_ge(C.gather[st.b], 32 * st.turn)
            pe.wait_ge(B.copied, G)
            dense(C, W2s, b2s, rows, c_ready)
            pe.wait_ge(C.edge, STEPS)
            pe.wait_ge(C.node, STEPS)
            scatter(D, True)
            pe.wait_ge(D.copied, G)

            def tick(at):
                st = at(2)
                if st.exists:
                    pe.wait_ge(e_hT, st.k + 1)
                    for m in range(HB):
                        if st.after(1):
                            pe.wait_ge(e_z1, st.k * HB + (m + 1 - HB))
                        pe.matmul(bank[m][:], w1x[:, m * P:(m + 1) * P], hT[:, 0, 0:4, :].rearrange("p s f -> p (s f)"),
                                  start=True, stop=False)
                        pe.matmul(bank[m][:], w1a[:, m * P:(m + 1) * P], aT[:], start=False, stop=True).then_inc(e_L1, 1)
                st = at(3)
                if st.exists:
                    pe.wait_ge(e_z2, st.k * HB + HB)
                    if st.after(1):
                        pe.wait_ge(e_out, st.k)
                    for s in range(T):
                        for c in range(HB):
                            last = pe.matmul(bank[4][:, s * P:(s + 1) * P], z2[:, c, s * P:(s + 1) * P], w3s[:, c, :],
                                             start=(c == 0), stop=(c == HB - 1))
                    last.then_inc(e_L3, 1)
                st = at(2)
                if st.exists:
                    pe.wait_ge(e_z1, st.k * HB + HB)
                    for m in range(HB):
                        if st.after(1):
                            pe.wait_ge(e_z2, st.k * HB + (m + 1 - HB))
                        for c in range(HB):
                            last = pe.matmul(bank[2 + m][:], w2s[:, c, m * P:(m + 1) * P], z1[:, c, :],
                                             start=(c == 0), stop=(c == HB - 1))
                        last.then_inc(e_L2, 1)
                st = at(1)
                if st.exists:
                    pe.wait_ge(e_normed, st.k + 1)
                    if st.after(1):
                        pe.wait_ge(e_hT, st.k)
                    for s in range(T):
                        pe.transpose(bank[5][:, s * P:(s + 1) * P], normed[:, st.b, s, :], ident[:])
                        last = pe.transpose(bank[6][0:FA, s * P:(s + 1) * P], node_out[:, st.b, s, F:ROW], ident[:])
                    last.then_inc(e_T, 1)
            ticks(pe, tick, 3)


_INS = ['x', 'src', 'dst', 'edge_attr_64', 'L0_gnn_W1', 'L0_gnn_b1', 'L0_gnn_W2', 'L0_gnn_b2', 'L1_gnn_u',
        'L1_gnn_w1', 'L1_gnn_b1', 'L1_gnn_w2', 'L1_gnn_b2', 'L1_gnn_w3', 'L1_gnn_b3']


def kernel(**inputs):
    import numpy as _np
    import concourse.bacc as _bacc
    from concourse import mybir as _mybir
    from concourse.bass_utils import run_bass_kernel_spmd as _run

    nc = _bacc.Bacc("TRN2", target_bir_lowering=False, num_devices=1)
    arrays, args = {}, []
    for name in _INS:
        a = _np.ascontiguousarray(inputs[name])
        arrays[f"in_{name}_dram"] = a
        args.append(nc.dram_tensor(f"in_{name}_dram", a.shape, _mybir.dt.from_np(a.dtype), kind="ExternalInput").ap())
    shape = arrays["in_x_dram"].shape
    args.append(nc.dram_tensor("out_0_dram", shape, _mybir.dt.from_np(_np.dtype('float32')), kind="ExternalOutput").ap())
    gnn_kernel(nc, *args)
    r = _run(nc, [arrays], core_ids=[0])
    return r.results[0]["out_0_dram"]
```

```python
from contextlib import ExitStack

import concourse.bass as bass
from concourse import mybir

ALU = mybir.AluOpType
ACT = mybir.ActivationFunctionType
F32 = mybir.dt.float32
F32R = mybir.dt.float32r
BF16 = mybir.dt.bfloat16
F16 = mybir.dt.float16
I32 = mybir.dt.int32

P = 128
EPS = 1e-5
SLOPE = 0.01


def gnn_kernel(nc, x, src, dst, edge_attr, W1, b1, W2, b2, u, w1, b1m, w2, b2m, w3, b3, out):
    N, F = x.shape
    E, FA = edge_attr.shape
    H = w1.shape[1]
    HB = H // P
    ROW = F + FA
    T = 4
    BLK = T * P
    EG = 2 * P
    G = (E + EG - 1) // EG
    GS = 2 * EG
    STEPS = 2 * G
    assert F == P and 2 * FA == P and (STEPS - 1) * BLK < N <= STEPS * BLK and STEPS % 4 == 0
    TAIL = E - (G - 1) * EG
    HI = STEPS * T
    NK = HI * P
    assert N + EG <= NK
    DUMP = NK
    NR = NK + GS
    HALF = HI // 2
    assert (NR - N) % 8 == 0 and (NR - N) // 8 <= P
    CH = 7
    CW = HI // CH
    assert CW * CH == HI and CW <= P and HALF <= 512

    pre1 = nc.dram_tensor("pre1", (NR, F), F32, kind="Internal").ap()
    node1 = nc.dram_tensor("node1", (NR, ROW), F32, kind="Internal").ap()
    msg1 = nc.dram_tensor("msg1", (G, P, 4, F), F32, kind="Internal").ap()
    msg2 = nc.dram_tensor("msg2", (G, P, 4, F), F32, kind="Internal").ap()
    keyrow = nc.dram_tensor("keyrow", (G, GS), F32, kind="Internal").ap()
    recip_in = nc.dram_tensor("recip_in", (NK, 1), F32, kind="Internal").ap()
    recip_out = nc.dram_tensor("recip_out", (NK, 1), F32, kind="Internal").ap()

    with ExitStack() as ctx:
        def sb(name, shape, dt=F32):
            return ctx.enter_context(nc.sbuf_tensor(name, shape, dt))

        def during(stage):
            return lambda name, shape, dt=F32: stage.enter_context(nc.sbuf_tensor(name, shape, dt))

        def sem(name):
            return ctx.enter_context(nc.semaphore(name))

        bank = [ctx.enter_context(nc.psum_tensor(f"bank{i}", [P, 512], F32)) for i in range(8)]

        ident = sb("ident", [P, P])
        later = sb("later", [P, GS])
        dumpcol = sb("dumpcol", [P, 4])
        W1s = sb("W1s", [P, 3, F])
        W2s = sb("W2s", [P, 3, F])
        b1col = sb("b1col", [P, 1])
        b2s = sb("b2s", [P, F])
        w1x = sb("w1x", [P, H])
        w1a = sb("w1a", [P, H])
        w1u = sb("w1u", [FA, H])
        u0 = sb("u0", [FA, 1])
        w2s = sb("w2s", [P, HB, H])
        w1x_hi, w1x_lo = sb("w1x_hi", [P, H], F32R), sb("w1x_lo", [P, H], F32R)
        w1a_hi, w1a_lo = sb("w1a_hi", [P, H], F32R), sb("w1a_lo", [P, H], F32R)
        w2_hi, w2_lo = sb("w2_hi", [P, HB, H], F32R), sb("w2_lo", [P, HB, H], F32R)
        w3s = sb("w3s", [P, HB, F])
        b3s = sb("b3s", [P, F])
        bias1 = sb("bias1", [P, HB])
        bias2 = sb("bias2", [P, HB])
        bias1_small = sb("bias1_small", [P, HB])
        bias2_small = sb("bias2_small", [P, HB])
        keys = sb("keys", [P, 2, 4, G])
        repkey = sb("repkey", [P, 4, G])
        recip = sb("recip", [P, 4, G])
        recip_buf = sb("recip_buf", [P, 4, 2])
        eps = sb("eps", [P, 1])
        rows = sb("rows", [P, 4, 6, F])
        resid = sb("resid", [P, 4, T, F])
        normed = sb("normed", [P, 4, 6, F])
        stats = sb("stats", [P, 4, 6, 6])
        moments = sb("moments", [P, 4, 6, 2])
        spread = sb("spread", [P, 4, 6])
        rstd = sb("rstd", [P, 4, 6])
        index = sb("index", [P, 4, 4], I32)
        hT = sb("hT", [P, 4, 6, P])
        node_out = sb("node_out", [P, 4, T, F + P])
        edge_out = sb("edge_out", [P, 4, 2, F])
        with ExitStack() as stage:
            own = during(stage)
            zeros = own("zeros", [P, 8 * ROW])
            iota_hi = own("iota_hi", [P, HI], F16)
            iota_lo = own("iota_lo", [P, P], F16)
            dumpi = own("dumpi", [P, 4], I32)
            ids_int = own("ids_int", [G, 2, EG], I32)
            ids = own("ids", [G, GS])
            keyi = own("keyi", [P, 4 * G], I32)
            part = own("part", [P, 2, 4 * G], I32)
            hilo = own("hilo", [P, 2, 4, G])
            onehot_hi = own("onehot_hi", [P, 4, HI], BF16)
            onehot_lo = own("onehot_lo", [P, 4, P], BF16)
            degree = own("degree", [P, 2, HI])
            degree_T = own("degree_T", [CW, 2, CH, P])
        with ExitStack() as stage:
            own = during(stage)
            group_msg = own("group_msg", [P, 2, 4, ROW])
            keyall = own("keyall", [P, 2, GS])
            same = own("same", [P, 2, 4, GS])
            masked = own("masked", [P, 4, GS])
            repeats = own("repeats", [P, 2, 4])
            todump = own("todump", [P, 2, 4])
            rep_index = own("rep_index", [P, 2, 4], I32)
            summed = own("summed", [P, 2, 4, ROW])
        with ExitStack() as stage:
            own = during(stage)
            h_hi, h_lo = own("h_hi", [P, BLK], F32R), own("h_lo", [P, BLK], F32R)
            a_parts = own("a_parts", [P, BLK], F32R)
            small1 = own("small1", [P, HB, BLK])
            z1 = own("z1", [P, 2, HB, BLK])
            z1_hi, z1_lo = own("z1_hi", [P, 2, HB, BLK], F32R), own("z1_lo", [P, 2, HB, BLK], F32R)
            small2 = own("small2", [P, HB, BLK])
            z2 = own("z2", [P, HB, BLK])

        block = ctx.enter_context(nc.Block())

        s_w = sem("weights_loaded")
        s_bias = sem("mlp_biases_loaded")
        s_pool_const = sem("pool_constants")
        s_pads = sem("ids_pads_written")
        s_ids = sem("ids_loaded")
        s_tails = sem("tail_rows_zeroed")
        s_idsf = sem("ids_as_floats")
        s_keyrow = sem("keyrow_stored")
        s_keysT = sem("keys_transposed")
        s_keys = sem("keys_ready")
        s_vprep = sem("vector_prelude_steps")
        s_onehot = sem("onehots_written")
        s_count = sem("onehots_counted")
        s_deg = sem("degrees_ready")
        s_degT = sem("degrees_transposed")
        s_degc = sem("degrees_copied")
        s_recip = sem("recip_tables_stored")
        s_ub = sem("u_product_ready")
        s_b1c = sem("bias_columns_ready")
        s_zcol = sem("attribute_columns_zeroed")
        s_kept = sem("recips_kept")

        class Dense:
            def __init__(self, n):
                self.load = [sem(f"{n}_rows_loaded{b}") for b in range(4)]
                self.index = sem(f"{n}_index_ready")
                self.gather = [sem(f"{n}_rows_gathered{b}") for b in range(4)]
                self.recip = [sem(f"{n}_recip_gathered{b}") for b in range(4)]
                self.stats = sem(f"{n}_stats")
                self.moments = sem(f"{n}_moments")
                self.spread = sem(f"{n}_spread")
                self.rstd = sem(f"{n}_rstd")
                self.normed = sem(f"{n}_normed")
                self.T = sem(f"{n}_transposed")
                self.hT = sem(f"{n}_hT_copied")
                self.resid = sem(f"{n}_resid_biased")
                self.mm = sem(f"{n}_products")
                self.edge = sem(f"{n}_edge_out_copied")
                self.node = sem(f"{n}_node_out_copied")
                self.store_node = [sem(f"{n}_node_stored{b}") for b in range(4)]
                self.store_edge = [sem(f"{n}_edge_stored{b}") for b in range(4)]

        class Scatter:
            def __init__(self, n):
                self.msg = [sem(f"{n}_messages_loaded{b}") for b in range(2)]
                self.keyall = [sem(f"{n}_keys_loaded{b}") for b in range(2)]
                self.same = sem(f"{n}_same_written")
                self.repeats = sem(f"{n}_repeats_counted")
                self.todump = sem(f"{n}_way_to_dump")
                self.moved = sem(f"{n}_offset_chosen")
                self.index = sem(f"{n}_index_ready")
                self.mm = sem(f"{n}_summed_product")
                self.copied = sem(f"{n}_sums_copied")
                self.done = [sem(f"{n}_added{b}") for b in range(2)]

        passed = {nc.scalar.engine: sem("scalar_waits_passed"), nc.vector.engine: sem("vector_waits_passed"), nc.gpsimd.engine: sem("pool_waits_passed")}
        A, C = Dense("a"), Dense("c")
        B, D = Scatter("b"), Scatter("d")
        e_load = [sem(f"e_rows_loaded{b}") for b in range(4)]
        e_store = [sem(f"e_out_stored{b}") for b in range(4)]
        e_stats, e_moments, e_spread = sem("e_stats"), sem("e_moments"), sem("e_spread")
        e_rstd, e_normed, e_resid = sem("e_rstd"), sem("e_normed"), sem("e_resid_biased")
        e_T, e_hi, e_ahi, e_lo = sem("e_transposed"), sem("e_h_hi"), sem("e_a_hi"), sem("e_h_and_a_lo")
        e_L1, e_small1, e_z1 = sem("e_L1"), sem("e_small1"), sem("e_z1")
        e_z1hi, e_z1lo = sem("e_z1_hi"), sem("e_z1_lo")
        s_whi, s_split = sem("weights_rounded"), sem("weights_split")
        e_L2, e_small2, e_z2 = sem("e_L2"), sem("e_small2"), sem("e_z2")
        e_L3, e_out = sem("e_L3"), sem("e_out")

        def sweep(eng, n, step):
            step(0)
            with eng.Fori(1, n - 1) as j:
                step(j)
            step(n - 1)

        class Step:

            def __init__(self, q, r):
                q, self.b = q + r // 4, r % 4
                self.k, self.turn, self.g, self.half = q * 4 + self.b, q + 1, q * 2 + self.b // 2, self.b % 2
                self.known = isinstance(q, int)
                self.exists = not self.known or 0 <= self.k < STEPS
                self.last = self.known and self.k == STEPS - 1

            def after(self, n):
                return not self.known or self.k >= n

        def ticks(eng, tick, lag):
            for t in range(8):
                tick(lambda n, t=t: Step(0, t - n))
            with eng.Fori(2, STEPS // 4 - 1) as q:
                for t in range(4):
                    tick(lambda n, t=t: Step(q, t - n))
            for t in range(4 + lag):
                tick(lambda n, t=t: Step(STEPS // 4 - 1, t - n))

        def hold(eng):
            eng.sem_inc(passed[eng.engine], 1)

        def before(g, n):
            return not isinstance(g, int) or g >= n

        def block_of(table, st):
            base = N - BLK if st.last else st.k * BLK
            return table[bass.ds(base, BLK), :].rearrange("(p t) f -> p t f", t=T)

        @block.sync
        def _(sp):
            for dst_ap, src_ap in ((W1s[:], W1.rearrange("(c p) f -> p c f", p=P)),
                                   (W2s[:], W2.rearrange("(c p) f -> p c f", p=P)),
                                   (b2s[:], b2.rearrange("(a f) -> a f", a=1).to_broadcast([P, F])),
                                   (w1x[:], w1[0:F, :]), (w1a[0:FA, :], w1[F:ROW, :]), (w1a[FA:P, :], w1[F:ROW, :]),
                                   (w1u[:], w1[ROW:ROW + FA, :]),
                                   (u0[:], u[0:1, :].rearrange("a f -> f a")),
                                   (w2s[:], w2.rearrange("(c p) f -> p c f", p=P)),
                                   (w3s[:], w3.rearrange("(c p) f -> p c f", p=P)),
                                   (b3s[:], b3.rearrange("(a f) -> a f", a=1).to_broadcast([P, F]))):
                sp.dma_start(dst_ap, src_ap).then_inc(s_w, 16)
            sp.wait_ge(s_pads, 1)
            for c, ends in enumerate((dst, src)):
                sp.dma_start(ids_int[0:G - 1, c, :],
                             ends[0:(G - 1) * EG].rearrange("(g e) -> g e", e=EG)).then_inc(s_ids, 16)
                sp.dma_start(ids_int[G - 1:G, c, 0:TAIL],
                             ends[(G - 1) * EG:E].rearrange("(g e) -> g e", g=1)).then_inc(s_ids, 16)
            for col, vec in ((bias1, b1m), (bias2, b2m), (b1col, b1)):
                sp.dma_start(col[:], vec.rearrange("(m p) -> p m", p=P), allow_slow_non_contiguous=True).then_inc(s_bias, 16)
            sp.wait_ge(s_pool_const, 1)
            for table, width in ((pre1, F), (node1, ROW)):
                sp.dma_start(table[N:NR, :].rearrange("(p r) f -> p (r f)", r=8), zeros[0:(NR - N) // 8, 0:8 * width])\
                    .then_inc(s_tails, 16)
            sp.wait_ge(s_idsf, 1)
            sp.dma_start(keyrow, ids[:]).then_inc(s_keyrow, 16)
            for c, table in enumerate((recip_in, recip_out)):
                sp.wait_ge(s_degc, c + 1)
                sp.dma_start(table.rearrange("(q r) a -> q (r a)", q=CW),
                             degree_T[:, c].rearrange("p c f -> p (c f)")).then_inc(s_recip, 16)

            def dense(S, source, with_x, target, width, msg):
                def tick(at):
                    st = at(0)
                    if st.exists:
                        if st.after(4):
                            sp.wait_ge(S.T if with_x else S.normed, st.k - 3)
                            if with_x:
                                sp.wait_ge(S.node, st.k - 3)
                        sp.dma_start(rows[:, st.b, 0:T, :], block_of(source, st)).then_inc(S.load[st.b], 16)
                        if with_x:
                            sp.dma_start(resid[:, st.b], block_of(x, st)).then_inc(S.load[st.b], 16)
                    st = at(3)
                    if st.exists:
                        sp.wait_ge(S.node, st.k + 1)
                        if st.last:
                            sp.wait_ge(S.store_node[st.b - 1], 16 * st.turn)
                        sp.dma_start(block_of(target, st), node_out[:, st.b, :, 0:width]).then_inc(S.store_node[st.b], 16)
                        sp.wait_ge(S.edge, st.k + 1)
                        sp.dma_start(msg[bass.ds(st.g, 1), :, st.half::2, :].rearrange("g p s f -> (g p) s f"),
                                     edge_out[:, st.b]).then_inc(S.store_edge[st.b], 16)
                ticks(sp, tick, 3)

            def scatter(S, X, msg, with_attr):
                if not with_attr:
                    sp.wait_ge(s_keyrow, 16)
                    sp.wait_ge(s_tails, 32)
                for b in range(4):
                    sp.wait_ge(X.store_edge[b], 16 * STEPS // 4)

                def step(g, b, uses):
                    if before(g, 2):
                        sp.wait_ge(S.mm, g - 1)
                    one = msg[bass.ds(g, 1)].rearrange("g p s f -> (g p) s f")
                    sp.dma_start(group_msg[:, b, :, 0:F], one).then_inc(S.msg[b], 16)
                    if with_attr:
                        if isinstance(g, int) and g == G - 1:
                            sp.dma_start(group_msg[:, b, 0, F:ROW], edge_attr[g * EG:g * EG + P, :]).then_inc(S.msg[b], 16)
                            sp.dma_start(group_msg[0:TAIL - P, b, 1, F:ROW], edge_attr[g * EG + P:E, :]).then_inc(S.msg[b], 16)
                        else:
                            for s in range(2):
                                sp.dma_start(group_msg[:, b, s, F:ROW], edge_attr[bass.ds(g * EG + s * P, P), :])\
                                    .then_inc(S.msg[b], 16)
                    sp.dma_start(keyall[:, b, :], keyrow[bass.ds(g, 1), :].to_broadcast([P, GS])).then_inc(S.keyall[b], 16)

                sweep(sp, G // 2, lambda j: [step(j * 2 + b, b, j + 1) for b in range(2)])

            dense(A, x, False, pre1, F, msg1)
            scatter(B, A, msg1, False)
            for b in range(2):
                sp.wait_ge(B.done[b], 64 * G // 2)
            dense(C, pre1, True, node1, ROW, msg2)
            scatter(D, C, msg2, True)
            for b in range(2):
                sp.wait_ge(D.done[b], 64 * G // 2)

            def tick(at):
                st = at(0)
                if st.exists:
                    if st.after(4):
                        sp.wait_ge(e_T, st.k - 3)
                        sp.wait_ge(e_resid, st.k - 3)
                    rows1 = block_of(node1, st)
                    sp.dma_start(node_out[:, st.b, :, 0:ROW], rows1).then_inc(e_load[st.b], 16)
                    sp.dma_start(node_out[:, st.b, :, ROW:F + P], rows1[:, :, F:ROW]).then_inc(e_load[st.b], 16)
                st = at(4)
                if st.exists:
                    sp.wait_ge(e_out, st.k + 1)
                    if st.last:
                        sp.wait_ge(e_store[st.b - 1], 16 * st.turn)
                    sp.dma_start(block_of(out, st), rows[:, st.b, 0:T, :]).then_inc(e_store[st.b], 16)
            ticks(sp, tick, 4)
            for b in range(4):
                sp.wait_ge(e_store[b], 16 * STEPS // 4)

        @block.gpsimd
        def _(pool):
            pool.memset(zeros[:], 0.0).then_inc(s_pool_const, 1)
            pool.iota(ids_int[:], pattern=[[0, 2], [1, EG]], base=N, channel_multiplier=0).then_inc(s_pads, 1)
            pool.memset(ident[:], 0.0).then_inc(s_pool_const, 1)
            pool.memset(later[:], 1.0).then_inc(s_pool_const, 1)
            pool.iota(iota_hi[:], pattern=[[1, HI]], base=0, channel_multiplier=0,
                      allow_small_or_imprecise_dtypes=True).then_inc(s_pool_const, 1)
            pool.iota(iota_lo[:], pattern=[[1, P]], base=0, channel_multiplier=0,
                      allow_small_or_imprecise_dtypes=True).then_inc(s_pool_const, 1)
            pool.iota(dumpi[:], pattern=[[P, 4]], base=DUMP, channel_multiplier=1).then_inc(s_pool_const, 1)
            pool.wait_ge(s_pool_const, 6)
            pool.affine_select(out=ident[:], in_=ident[:], compare_op=ALU.not_equal, fill=1.0, base=0,
                               pattern=[[-1, P]], channel_multiplier=1).then_inc(s_pool_const, 1)
            pool.affine_select(out=later[:], in_=later[:], compare_op=ALU.is_gt, fill=0.0, base=0,
                               pattern=[[1, GS]], channel_multiplier=-1).then_inc(s_pool_const, 1)
            pool.tensor_copy(dumpcol[:], dumpi[:]).then_inc(s_pool_const, 1)
            pool.memset(node_out[:], 0.0).then_inc(s_zcol, 1)

            def dense(S, table, with_recip):
                def tick(at):
                    st = at(0)
                    b = st.b
                    if st.after(4):
                        pool.wait_ge(S.normed if with_recip else S.T, st.k - 3)
                    pool.wait_ge(S.index, st.k + 1)
                    hold(pool)
                    for slot, col in ((T, 1), (T + 1, 0)):
                        pool.indirect_dma_start(rows[:, b, slot, :], None, table,
                                                bass.IndirectOffsetOnAxis(ap=index[:, b, col:col + 1], axis=0))\
                            .then_inc(S.gather[b], 16)
                    if with_recip:
                        if st.after(4):
                            pool.wait_ge(s_kept, st.k - 3)
                        hold(pool)
                        for slot, tab in enumerate((recip_in, recip_out)):
                            pool.indirect_dma_start(recip_buf[:, b, slot:slot + 1], None, tab,
                                                    bass.IndirectOffsetOnAxis(ap=index[:, b, 2 + slot:3 + slot], axis=0))\
                                .then_inc(S.recip[b], 16)
                ticks(pool, tick, 0)

            def scatter(S, X, target, width):
                for b in range(4):
                    pool.wait_ge(X.store_node[b], 16 * STEPS // 4)
                pool.wait_ge(s_tails, 32)

                def step(g, b, uses):
                    pool.wait_ge(S.copied, g + 1)
                    pool.wait_ge(S.index, g + 1)
                    if before(g, 1):
                        last = (uses - 1) if b == 0 else uses
                        pool.wait_ge(S.done[1 - b], last * 64)
                    hold(pool)
                    for s in range(4):
                        pool.indirect_dma_start(target, bass.IndirectOffsetOnAxis(ap=rep_index[:, b, s:s + 1], axis=0),
                                                summed[:, b, s, 0:width], None, compute_op=ALU.add).then_inc(S.done[b], 16)

                sweep(pool, G // 2, lambda j: [step(j * 2 + b, b, j + 1) for b in range(2)])

            pool.wait_ge(s_recip, 32)
            dense(A, x, True)
            scatter(B, A, pre1, F)
            for b in range(2):
                pool.wait_ge(B.done[b], 64 * G // 2)
            dense(C, pre1, False)
            scatter(D, C, node1, ROW)

            def tick(at):
                st = at(0)
                if st.exists:
                    b = st.b
                    pool.wait_ge(e_load[b], 32 * st.turn)
                    if st.after(4):
                        pool.wait_ge(e_out, st.k - 3)
                    for s in range(T):
                        last = pool.tensor_tensor(resid[:, b, s, :], node_out[:, b, s, 0:F], b3s[:], ALU.add)
                    last.then_inc(e_resid, 1)
                st = at(2)
                if st.exists:
                    for m in range(HB):
                        pool.wait_ge(e_z1hi, st.k * HB + (m + 1))
                        if st.after(2):
                            pool.wait_ge(e_L2, st.k * HB + (HB - 2 * HB))
                        pool.tensor_tensor(z1_lo[:, st.b % 2, m, :], z1[:, st.b % 2, m, :], z1_hi[:, st.b % 2, m, :].bitcast(F32),
                                           ALU.subtract).then_inc(e_z1lo, 1)
            ticks(pool, tick, 2)

        @block.scalar
        def _(act):
            act.wait_ge(s_keys, 1)

            def stage_index(S, st):
                if st.after(4):
                    act.wait_ge(S.gather[st.b], 32 * (st.turn - 1))
                act.activation(index[:, st.b, :].rearrange("p (a s) -> p a s", a=2),
                               keys[:, :, st.half::2, bass.ds(st.g, 1)].rearrange("p a s g -> p a (s g)"),
                               ACT.Copy).then_inc(S.index, 1)

            def copy_hT(S, st):
                bias = b1col[:, 0:1] if S is C else 0.0
                act.wait_ge(S.T, st.k + 1)
                o = 2 * (st.b % 2)
                act.activation(hT[:, st.b, 0:4, :].rearrange("p s f -> p (s f)"), bank[o][:], ACT.Relu, bias=bias)
                act.activation(hT[:, st.b, 4:6, :].rearrange("p s f -> p (s f)"), bank[o + 1][:, 0:2 * P], ACT.Relu,
                               bias=bias)\
                    .then_inc(S.hT, 1)

            def copy_edge(S, st):
                if st.after(4):
                    act.wait_ge(S.store_edge[st.b], 16 * (st.turn - 1))
                    hold(act)
                for s in range(2):
                    last = act.activation(edge_out[:, st.b, s, :], bank[5 + 2 * (st.b % 2)][:, s * P:(s + 1) * P],
                                          ACT.Copy, scale=recip[:, st.half + 2 * s, bass.ds(st.g, 1)])
                last.then_inc(S.edge, 1)

            act.wait_ge(s_zcol, 2)
            for k in range(3):
                stage_index(A, Step(0, k))

            def tick(at):
                st = at(1)
                if st.exists:
                    act.wait_ge(A.recip[st.b], 32 * st.turn)
                    act.activation(recip[:, st.half::2, bass.ds(st.g, 1)].rearrange("p s g -> p (s g)"),
                                   recip_buf[:, st.b, :], ACT.Copy).then_inc(s_kept, 1)
                    copy_hT(A, st)
                st = at(0)
                if st.exists:
                    act.wait_ge(A.moments, st.k + 1)
                    act.activation(spread[:, st.b, :], moments[:, st.b, :, 1], ACT.Sqrt, bias=eps[:, 0:1]).then_inc(A.spread, 1)
                st = at(2)
                if st.exists:
                    act.wait_ge(A.mm, st.k + 1)
                    if st.after(4):
                        act.wait_ge(A.store_node[st.b], 16 * (st.turn - 1))
                    act.activation(node_out[:, st.b, :, 0:F], bank[4 + 2 * (st.b % 2)][:].rearrange("p (t f) -> p t f", t=T),
                                   ACT.Copy).then_inc(A.node, 1)
                    act.wait_ge(s_kept, st.k + 1)
                    copy_edge(A, st)
                st = at(-3)
                if st.exists:
                    stage_index(A, st)
            ticks(act, tick, 2)

            def scatter(S, width):
                def step(g, b, uses):
                    act.wait_ge(S.mm, g + 1)
                    if before(g, 2):
                        act.wait_ge(S.done[b], 64 * (uses - 1))
                    if S is D:
                        act.activation(rep_index[:, b, :], repkey[:, :, bass.ds(g, 1)].rearrange("p s g -> p (s g)"),
                                       ACT.Copy).then_inc(S.index, 1)
                    for c in range(2):
                        last = act.activation(summed[:, b, 2 * c:2 * c + 2, 0:width],
                                              bank[4 + 2 * b + c][:].rearrange("p (s f) -> p s f", s=2)[:, :, 0:width],
                                              ACT.Copy)
                    last.then_inc(S.copied, 1)
                sweep(act, G // 2, lambda j: [step(j * 2 + b, b, j + 1) for b in range(2)])

            scatter(B, F)

            for k in range(3):
                stage_index(C, Step(0, k))

            def tick(at):
                st = at(-3)
                if st.exists:
                    stage_index(C, st)
                st = at(1)
                if st.exists:
                    copy_hT(C, st)
                st = at(2)
                if st.exists:
                    act.wait_ge(C.mm, st.k + 1)
                    copy_edge(C, st)
            act.wait_ge(s_kept, STEPS)
            ticks(act, tick, 2)
            scatter(D, ROW)

            act.wait_ge(s_b1c, 4)

            def scaled(st, products, first_bank, bias_small, small, ready):
                for m in range(HB):
                    act.wait_ge(products, st.k * HB + (m + 1))
                    act.activation(small[:, m, :], bank[first_bank + m][:], ACT.Identity, scale=SLOPE,
                                   bias=bias_small[:, m:m + 1]).then_inc(ready, 1)

            def tick(at):
                st = at(4)
                if st.exists:
                    scaled(st, e_L2, 2, bias2_small, small2, e_small2)
                st = at(2)
                if st.exists:
                    scaled(st, e_L1, 0, bias1_small, small1, e_small1)
                st = at(1)
                if st.exists:
                    act.wait_ge(e_T, st.k + 1)
                    act.activation(h_hi[:], bank[5][:], ACT.Relu).then_inc(e_hi, 1)
                    act.activation(a_parts[:], bank[6][:], ACT.Copy).then_inc(e_ahi, 1)
                st = at(2)
                if st.exists:
                    for m in range(HB):
                        act.wait_ge(e_z1, st.k * HB + (m + 1))
                        if st.after(2):
                            act.wait_ge(e_L2, st.k * HB + (HB - 2 * HB))
                        act.activation(z1_hi[:, st.b % 2, m, :], z1[:, st.b % 2, m, :], ACT.Copy).then_inc(e_z1hi, 1)
                st = at(0)
                if st.exists:
                    act.wait_ge(e_moments, st.k + 1)
                    act.activation(spread[:, st.b, 0:T], moments[:, st.b, 0:T, 1], ACT.Sqrt, bias=eps[:, 0:1])\
                        .then_inc(e_spread, 1)
            ticks(act, tick, 4)

        @block.vector
        def _(dve):
            dve.memset(eps[:], EPS).then_inc(s_zcol, 1)
            dve.wait_ge(s_ids, 64)
            dve.tensor_copy(ids[:], ids_int[:].rearrange("g c e -> g (c e)")).then_inc(s_idsf, 1)
            kk = keys[:, 1].rearrange("p s g -> p (s g)")
            dve.wait_ge(s_keysT, 1)
            dve.tensor_copy(kk, bank[0][:, 0:4 * G]).then_inc(s_vprep, 1)
            dve.wait_ge(s_vprep, 1)
            dve.tensor_scalar(keys[:, 0].rearrange("p s g -> p (s g)"), kk, float(N - 1), None, ALU.min).then_inc(s_keys, 1)
            dve.tensor_copy(keyi[:], kk).then_inc(s_vprep, 1)
            dve.wait_ge(s_vprep, 2)
            dve.tensor_scalar(part[:, 0], keyi[:], 7, None, ALU.logical_shift_right).then_inc(s_vprep, 1)
            dve.tensor_scalar(part[:, 1], keyi[:], P - 1, None, ALU.bitwise_and).then_inc(s_vprep, 1)
            dve.wait_ge(s_vprep, 4)
            dve.tensor_copy(hilo[:].rearrange("p a s g -> p a (s g)"), part[:]).then_inc(s_vprep, 1)
            dve.wait_ge(s_vprep, 5)
            dve.wait_ge(s_pool_const, 9)

            def onehots(g):
                for s in range(4):
                    if before(g, 1):
                        dve.wait_ge(s_count, g * 4 + s - 3)
                    dve.tensor_scalar(onehot_lo[:, s, :], iota_lo[:], hilo[:, 1, s, bass.ds(g, 1)], None, ALU.is_equal)
                    dve.tensor_scalar(onehot_hi[:, s, :], iota_hi[:], hilo[:, 0, s, bass.ds(g, 1)], None, ALU.is_equal)\
                        .then_inc(s_onehot, 1)
            sweep(dve, G, onehots)
            dve.wait_ge(s_count, 4 * G)
            for c in range(2):
                for h in range(2):
                    last = dve.tensor_scalar(degree[:, c, h * HALF:(h + 1) * HALF], bank[2 * c + h][:, 0:HALF], 1.0, None, ALU.max)
            last.then_inc(s_vprep, 1)
            dve.wait_ge(s_vprep, 6)
            dve.reciprocal(degree[:], degree[:]).then_inc(s_deg, 1)
            for c in range(2):
                dve.wait_ge(s_degT, c + 1)
                dve.tensor_copy(degree_T[:, c, 0:4, :], bank[4 + 2 * c][0:CW, :].rearrange("p (c f) -> p c f", f=P))
                dve.tensor_copy(degree_T[:, c, 4:CH, :], bank[5 + 2 * c][0:CW, 0:(CH - 4) * P].rearrange("p (c f) -> p c f", f=P))\
                    .then_inc(s_degc, 1)
            dve.wait_ge(s_w, 16 * 11)
            pairs = ((w1x, w1x_hi, w1x_lo), (w1a, w1a_hi, w1a_lo), (w2s, w2_hi, w2_lo))
            for w, hi, _ in pairs:
                dve.tensor_copy(hi[:], w[:]).then_inc(s_whi, 1)
            dve.wait_ge(s_whi, len(pairs))
            for w, hi, lo in pairs:
                dve.tensor_tensor(lo[:], w[:], hi[:].bitcast(F32), ALU.subtract).then_inc(s_split, 1)
            dve.wait_ge(s_ub, 1)
            dve.wait_ge(s_bias, 48)
            dve.tensor_tensor(bias1[:], bank[0][:, 0:HB], bias1[:], ALU.add).then_inc(s_b1c, 1)
            dve.wait_ge(s_b1c, 1)
            dve.tensor_scalar(bias1_small[:], bias1[:], SLOPE, None, ALU.mult).then_inc(s_b1c, 1)
            dve.tensor_scalar(bias2_small[:], bias2[:], SLOPE, None, ALU.mult).then_inc(s_b1c, 2)

            def moments_of(sems, st, n, source):
                s_stats, s_moments = sems
                for s in range(n):
                    last = dve.bn_stats(stats[:, st.b, s, :], source(st.b, s))
                last.then_inc(s_stats, 1)
                dve.wait_ge(s_stats, st.k + 1)
                hold(dve)
                for s in range(n):
                    last = dve.bn_aggr(moments[:, st.b, s, :], stats[:, st.b, s, :])
                last.then_inc(s_moments, 1)

            def normalise(sems, st, n, source):
                s_spread, s_rstd, s_normed, s_read = sems
                dve.wait_ge(s_spread, st.k + 1)
                dve.reciprocal(rstd[:, st.b, 0:n], spread[:, st.b, 0:n]).then_inc(s_rstd, 1)
                if st.after(4):
                    dve.wait_ge(s_read, st.k - 3)
                dve.wait_ge(s_rstd, st.k + 1)
                for s in range(n):
                    last = dve.tensor_scalar(normed[:, st.b, s, :], source(st.b, s), moments[:, st.b, s, 0:1],
                                             rstd[:, st.b, s:s + 1], ALU.subtract, ALU.mult)
                last.then_inc(s_normed, 1)

            def tick(at):
                st = at(1)
                if st.exists:
                    normalise((A.spread, A.rstd, A.normed, A.T), st, 6, lambda b, s: rows[:, b, s, :])
                st = at(0)
                if st.exists:
                    dve.wait_ge(A.load[st.b], 16 * st.turn)
                    dve.wait_ge(A.gather[st.b], 32 * st.turn)
                    moments_of((A.stats, A.moments), st, 6, lambda b, s: rows[:, b, s, :])
            ticks(dve, tick, 1)

            def scatter(S):
                def step(g, b, uses):
                    dve.wait_ge(S.keyall[b], 16 * uses)
                    if before(g, 2):
                        dve.wait_ge(S.mm, g - 1)
                    for s in range(4):
                        last = dve.tensor_scalar(same[:, b, s, s * P:GS], keyall[:, b, s * P:GS],
                                                 keys[:, 1, s, bass.ds(g, 1)], None, ALU.is_equal)
                    last.then_inc(S.same, 1)
                    if S is D:
                        return
                    dve.wait_ge(S.same, g + 1)
                    for s in range(4):
                        last = dve.tensor_tensor_reduce(masked[:, s, s * P:GS], same[:, b, s, s * P:GS], later[:, 0:GS - s * P],
                                                        1.0, 0.0, ALU.mult, ALU.add, repeats[:, b, s:s + 1])
                    dve.tensor_tensor(todump[:, b, :], dumpcol[:], keys[:, 1, :, bass.ds(g, 1)].rearrange("p s g -> p (s g)"),
                                      ALU.subtract).then_inc(S.todump, 1)
                    dve.wait_ge(S.todump, g + 1)
                    dve.scalar_tensor_tensor(out=todump[:, b, :], in0=repeats[:, b, :], scalar=0.0, in1=todump[:, b, :],
                                             op0=ALU.is_gt, op1=ALU.mult).then_inc(S.moved, 1)
                    dve.wait_ge(S.moved, g + 1)
                    rk = repkey[:, :, bass.ds(g, 1)].rearrange("p s g -> p (s g)")
                    dve.tensor_tensor(rk, keys[:, 1, :, bass.ds(g, 1)].rearrange("p s g -> p (s g)"), todump[:, b, :], ALU.add)\
                        .then_inc(S.repeats, 1)
                    if before(g, 2):
                        dve.wait_ge(S.done[b], 64 * (uses - 1))
                    dve.wait_ge(S.repeats, g + 1)
                    dve.tensor_scalar(rep_index[:, b, :], rk, 0.0, None, ALU.add).then_inc(S.index, 1)
                sweep(dve, G // 2, lambda j: [step(j * 2 + b, b, j + 1) for b in range(2)])
            scatter(B)

            def tick(at):
                st = at(1)
                if st.exists:
                    dve.wait_ge(C.load[st.b], 32 * st.turn)
                    dve.tensor_tensor(resid[:, st.b], resid[:, st.b], b2s[:].unsqueeze(1).to_broadcast([P, T, F]), ALU.add)\
                        .then_inc(C.resid, 1)
                st = at(2)
                if st.exists:
                    dve.wait_ge(C.mm, st.k + 1)
                    dve.wait_ge(C.resid, st.k + 1)
                    if st.after(4):
                        dve.wait_ge(C.store_node[st.b], 16 * (st.turn - 1))
                    dve.tensor_tensor(node_out[:, st.b, :, 0:F], bank[4 + 2 * (st.b % 2)][:].rearrange("p (t f) -> p t f", t=T),
                                      resid[:, st.b], ALU.add).then_inc(C.node, 1)
            ticks(dve, tick, 2)
            scatter(D)

            def leaky(st, small_ready, first_bank, bias, small, z, ready):
                for m in range(HB):
                    dve.wait_ge(small_ready, st.k * HB + (m + 1))
                    dve.scalar_tensor_tensor(out=z[:, m, :], in0=bank[first_bank + m][:], scalar=bias[:, m:m + 1],
                                             in1=small[:, m, :], op0=ALU.add, op1=ALU.max).then_inc(ready, 1)

            def tick(at):
                st = at(1)
                if st.exists:
                    normalise((e_spread, e_rstd, e_normed, e_T), st, T, lambda b, s: node_out[:, b, s, 0:F])
                st = at(4)
                if st.exists:
                    leaky(st, e_small2, 2, bias2, small2, z2, e_z2)
                st = at(2)
                if st.exists:
                    if st.after(2):
                        dve.wait_ge(e_z1lo, st.k * HB - HB)
                    leaky(st, e_small1, 0, bias1, small1, z1[:, st.b % 2], e_z1)
                st = at(1)
                if st.exists:
                    dve.wait_ge(e_hi, st.k + 1)
                    dve.scalar_tensor_tensor(out=h_lo[:], in0=bank[5][:], scalar=0.0, in1=h_hi[:].bitcast(F32),
                                             op0=ALU.max, op1=ALU.subtract)
                    dve.wait_ge(e_ahi, st.k + 1)
                    dve.tensor_tensor(a_parts[FA:P, :], bank[6][FA:P, :], a_parts[FA:P, :].bitcast(F32), ALU.subtract)\
                        .then_inc(e_lo, 1)
                st = at(0)
                if st.exists:
                    dve.wait_ge(e_load[st.b], 32 * st.turn)
                    moments_of((e_stats, e_moments), st, T, lambda b, s: node_out[:, b, s, 0:F])
                st = at(4)
                if st.exists:
                    dve.wait_ge(e_L3, st.k + 1)
                    dve.wait_ge(e_resid, st.k + 1)
                    if st.after(4):
                        dve.wait_ge(e_store[st.b], 16 * (st.turn - 1))
                    dve.tensor_tensor(rows[:, st.b, 0:T, :], bank[4][:].rearrange("p (t f) -> p t f", t=T),
                                      resid[:, st.b], ALU.add).then_inc(e_out, 1)
            ticks(dve, tick, 4)

        @block.tensor
        def _(pe):
            pe.wait_ge(s_pool_const, 9)
            pe.wait_ge(s_idsf, 1)
            for s in range(4):
                last = pe.transpose(bank[0][:, s * G:(s + 1) * G], ids[:, s * P:(s + 1) * P], ident[0:G, 0:G])
            last.then_inc(s_keysT, 1)
            pe.wait_ge(s_keys, 1)

            def count(g):
                for s in range(4):
                    pe.wait_ge(s_onehot, g * 4 + s + 1)
                    for h in range(2):
                        last = pe.matmul(bank[2 * (s // 2) + h][:, 0:HALF], onehot_lo[:, s, :],
                                         onehot_hi[:, s, h * HALF:(h + 1) * HALF],
                                         start=(isinstance(g, int) and g == 0 and s % 2 == 0),
                                         stop=(isinstance(g, int) and g == G - 1 and s % 2 == 1))
                    last.then_inc(s_count, 1)
            sweep(pe, G, count)
            pe.wait_ge(s_deg, 1)
            for c in range(2):
                cols = degree[:, c].rearrange("p (q r) -> p r q", r=CH)
                for r in range(CH):
                    last = pe.transpose(bank[4 + 2 * c + r // 4][0:CW, (r % 4) * P:(r % 4 + 1) * P], cols[:, r, :], ident[:])
                last.then_inc(s_degT, 1)
            pe.wait_ge(s_w, 16 * 11)
            for m in range(HB):
                last = pe.matmul(bank[0][:, m:m + 1], w1u[:, m * P:(m + 1) * P], u0[:], start=True, stop=True)
            last.then_inc(s_ub, 1)

            def dense(S, W, source, ready):
                def tick(at):
                    st = at(1)
                    if st.exists:
                        ready(st)
                        if st.after(2):
                            pe.wait_ge(S.hT, st.k - 1)
                        for s in range(6):
                            last = pe.transpose(bank[s // 4 + 2 * (st.b % 2)][:, (s % 4) * P:(s % 4 + 1) * P],
                                                source[:, st.b, s, :], ident[:])
                        last.then_inc(S.T, 1)
                    st = at(2)
                    if st.exists:
                        pe.wait_ge(S.hT, st.k + 1)
                        if st.after(2):
                            pe.wait_ge(S.node, st.k - 1)
                            pe.wait_ge(S.edge, st.k - 1)
                        for s in range(T):
                            o = bank[4 + 2 * (st.b % 2)][:, s * P:(s + 1) * P]
                            pe.matmul(o, hT[:, st.b, s, :], W[:, 0, :], start=True, stop=True)
                        for s in range(2):
                            last = pe.matmul(bank[5 + 2 * (st.b % 2)][:, s * P:(s + 1) * P], hT[:, st.b, T + s, :],
                                             W[:, 1 + s, :], start=True, stop=True)
                        last.then_inc(S.mm, 1)
                ticks(pe, tick, 2)

            def scatter(S, with_attr):
                def step(g, b, uses):
                    pe.wait_ge(S.same, g + 1)
                    pe.wait_ge(S.msg[b], (48 if with_attr else 16) * uses)
                    if before(g, 2):
                        pe.wait_ge(S.copied, g - 1)
                    for i in range(4):
                        for j in range(i + 1):
                            w = ROW if with_attr and j < 2 else F
                            o = bank[4 + 2 * b + i // 2][:, (i % 2) * 256:(i % 2) * 256 + w]
                            last = pe.matmul(o, same[:, b, j, i * P:(i + 1) * P], group_msg[:, b, j, 0:w],
                                             start=(j == 0), stop=(j == i))
                    last.then_inc(S.mm, 1)
                sweep(pe, G // 2, lambda j: [step(j * 2 + b, b, j + 1) for b in range(2)])

            pe.wait_ge(s_degc, 2)
            pe.wait_ge(s_b1c, 1)
            dense(A, W1s, normed, lambda st: pe.wait_ge(A.normed, st.k + 1))
            pe.wait_ge(A.edge, STEPS)
            scatter(B, False)

            def c_ready(st):
                pe.wait_ge(C.load[st.b], 32 * st.turn)
                pe.wait_ge(C.gather[st.b], 32 * st.turn)
            pe.wait_ge(B.copied, G)
            dense(C, W2s, rows, c_ready)
            pe.wait_ge(C.edge, STEPS)
            pe.wait_ge(C.node, STEPS)
            scatter(D, True)
            pe.wait_ge(D.copied, G)

            def tick(at):
                st = at(2)
                if st.exists:
                    pe.wait_ge(e_lo, st.k + 1)
                    for m in range(HB):
                        c = slice(m * P, (m + 1) * P)
                        if st.after(1):
                            pe.wait_ge(e_z1, st.k * HB + (m + 1 - HB))
                        pe.matmul(bank[m][:], w1x_hi[:, c], h_hi[:], start=True, stop=False)
                        pe.matmul(bank[m][:], w1x_hi[:, c], h_lo[:], start=False, stop=False)
                        pe.matmul(bank[m][:], w1x_lo[:, c], h_hi[:], start=False, stop=False)
                        pe.matmul(bank[m][:], w1a_hi[:, c], a_parts[:], start=False, stop=False)
                        pe.matmul(bank[m][:], w1a_lo[0:FA, c], a_parts[0:FA, :], start=False, stop=True).then_inc(e_L1, 1)
                st = at(1)
                if st.exists:
                    pe.wait_ge(e_normed, st.k + 1)
                    if st.after(1):
                        pe.wait_ge(e_lo, st.k)
                    for s in range(T):
                        pe.transpose(bank[5][:, s * P:(s + 1) * P], normed[:, st.b, s, :], ident[:])
                        last = pe.transpose(bank[6][:, s * P:(s + 1) * P],
                                            node_out[:, st.b, s, F:F + P], ident[:])
                    last.then_inc(e_T, 1)
                st = at(4)
                if st.exists:
                    pe.wait_ge(e_z2, st.k * HB + HB)
                    if st.after(1):
                        pe.wait_ge(e_out, st.k)
                    for s in range(T):
                        for c in range(HB):
                            last = pe.matmul(bank[4][:, s * P:(s + 1) * P], z2[:, c, s * P:(s + 1) * P], w3s[:, c, :],
                                             start=(c == 0), stop=(c == HB - 1))
                    last.then_inc(e_L3, 1)
                st = at(3)
                if st.exists:
                    pe.wait_ge(e_z1lo, st.k * HB + HB)
                    d = st.b % 2
                    for m in range(HB):
                        cols = slice(m * P, (m + 1) * P)
                        if st.after(1):
                            pe.wait_ge(e_z2, st.k * HB + (m + 1 - HB))
                        for c in range(HB):
                            pe.matmul(bank[2 + m][:], w2_hi[:, c, cols], z1_hi[:, d, c, :], start=(c == 0), stop=False)
                            pe.matmul(bank[2 + m][:], w2_hi[:, c, cols], z1_lo[:, d, c, :], start=False, stop=False)
                            last = pe.matmul(bank[2 + m][:], w2_lo[:, c, cols], z1_hi[:, d, c, :], start=False,
                                             stop=(c == HB - 1))
                        last.then_inc(e_L2, 1)
            pe.wait_ge(s_split, 3)
            ticks(pe, tick, 4)


_INS = ['x', 'src', 'dst', 'edge_attr_64', 'L0_gnn_W1', 'L0_gnn_b1', 'L0_gnn_W2', 'L0_gnn_b2', 'L1_gnn_u',
        'L1_gnn_w1', 'L1_gnn_b1', 'L1_gnn_w2', 'L1_gnn_b2', 'L1_gnn_w3', 'L1_gnn_b3']


def kernel(**inputs):
    import numpy as _np
    import concourse.bacc as _bacc
    from concourse import mybir as _mybir
    from concourse.bass_utils import run_bass_kernel_spmd as _run

    nc = _bacc.Bacc("TRN2", target_bir_lowering=False, num_devices=1)
    arrays, args = {}, []
    for name in _INS:
        a = _np.ascontiguousarray(inputs[name])
        arrays[f"in_{name}_dram"] = a
        args.append(nc.dram_tensor(f"in_{name}_dram", a.shape, _mybir.dt.from_np(a.dtype), kind="ExternalInput").ap())
    shape = arrays["in_x_dram"].shape
    args.append(nc.dram_tensor("out_0_dram", shape, _mybir.dt.from_np(_np.dtype('float32')), kind="ExternalOutput").ap())
    gnn_kernel(nc, *args)
    r = _run(nc, [arrays], core_ids=[0])
    return r.results[0]["out_0_dram"]
```

```python
from contextlib import ExitStack

import concourse.bass as bass
from concourse import mybir

ALU = mybir.AluOpType
ACT = mybir.ActivationFunctionType
F32 = mybir.dt.float32
F32R = mybir.dt.float32r
BF16 = mybir.dt.bfloat16
F16 = mybir.dt.float16
I32 = mybir.dt.int32

P = 128
EPS = 1e-5
SLOPE = 0.01


def gnn_kernel(nc, x, src, dst, edge_attr, W1, b1, W2, b2, u, w1, b1m, w2, b2m, w3, b3, out):
    N, F = x.shape
    E, FA = edge_attr.shape
    H = w1.shape[1]
    HB = H // P
    ROW = F + FA
    T = 4
    BLK = T * P
    EG = 2 * P
    G = (E + EG - 1) // EG
    GS = 2 * EG
    STEPS = 2 * G
    assert F == P and 2 * FA == P and (STEPS - 1) * BLK < N <= STEPS * BLK and STEPS % 4 == 0
    TAIL = E - (G - 1) * EG
    HI = STEPS * T
    NK = HI * P
    assert N + EG <= NK
    DUMP = NK
    NR = NK + GS
    HALF = HI // 2
    assert (NR - N) % 8 == 0 and (NR - N) // 8 <= P and NR % (4 * P) == 0
    CH = 7
    CW = HI // CH
    assert CW * CH == HI and CW <= P and HALF <= 512

    pre1 = nc.dram_tensor("pre1", (NR, F), F32, kind="Internal").ap()
    node1 = nc.dram_tensor("node1", (NR, ROW), F32, kind="Internal").ap()
    msg1 = nc.dram_tensor("msg1", (G, P, 4, F), F32, kind="Internal").ap()
    msg2 = nc.dram_tensor("msg2", (G, P, 2, F), F32, kind="Internal").ap()
    keyrow = nc.dram_tensor("keyrow", (G, GS), F32, kind="Internal").ap()
    recip_in = nc.dram_tensor("recip_in", (NK, 1), F32, kind="Internal").ap()
    recip_out = nc.dram_tensor("recip_out", (NK, 1), F32, kind="Internal").ap()

    with ExitStack() as ctx:
        def sb(name, shape, dt=F32):
            return ctx.enter_context(nc.sbuf_tensor(name, shape, dt))

        def during(stage):
            return lambda name, shape, dt=F32: stage.enter_context(nc.sbuf_tensor(name, shape, dt))

        def sem(name):
            return ctx.enter_context(nc.semaphore(name))

        bank = [ctx.enter_context(nc.psum_tensor(f"bank{i}", [P, 512], F32)) for i in range(8)]

        ident = sb("ident", [P, P])
        later = sb("later", [P, GS])
        dumpcol = sb("dumpcol", [P, 4])
        W1s = sb("W1s", [P, 3, F])
        W2s = sb("W2s", [P, 3, F])
        b1col = sb("b1col", [P, 1])
        b2s = sb("b2s", [P, F])
        w1x = sb("w1x", [P, H])
        w1a = sb("w1a", [P, H])
        w1u = sb("w1u", [FA, H])
        u0 = sb("u0", [FA, 1])
        w2s = sb("w2s", [P, HB, H])
        w1x_hi, w1x_lo = sb("w1x_hi", [P, H], F32R), sb("w1x_lo", [P, H], F32R)
        w1a_hi, w1a_lo = sb("w1a_hi", [P, H], F32R), sb("w1a_lo", [P, H], F32R)
        w2_hi, w2_lo = sb("w2_hi", [P, HB, H], F32R), sb("w2_lo", [P, HB, H], F32R)
        w3s = sb("w3s", [P, HB, F])
        b3s = sb("b3s", [P, F])
        bias1 = sb("bias1", [P, HB])
        bias2 = sb("bias2", [P, HB])
        bias1_small = sb("bias1_small", [P, HB])
        bias2_small = sb("bias2_small", [P, HB])
        keys = sb("keys", [P, 2, 4, G])
        repkey = sb("repkey", [P, 4, G])
        recip = sb("recip", [P, 4, G])
        recip_buf = sb("recip_buf", [P, 4, 2])
        eps = sb("eps", [P, 1])
        rows = sb("rows", [P, 4, 6, F])
        resid = sb("resid", [P, 4, T, F])
        normed = sb("normed", [P, 4, 6, F])
        stats = sb("stats", [P, 4, 6, 6])
        moments = sb("moments", [P, 4, 6, 2])
        spread = sb("spread", [P, 4, 6])
        rstd = sb("rstd", [P, 4, 6])
        index = sb("index", [P, 4, 4], I32)
        hT = sb("hT", [P, 4, 6, P])
        node_out = sb("node_out", [P, 4, T, F + P])
        edge_out = sb("edge_out", [P, 4, 2, F])
        negmean = sb("negmean", [P, 4, 2])
        endscale = sb("endscale", [P, 4])
        with ExitStack() as stage:
            own = during(stage)
            zeros = own("zeros", [P, 8 * F])
            iota_hi = own("iota_hi", [P, HALF], F16)
            iota_lo = own("iota_lo", [P, 2 * P], F16)
            dumpi = own("dumpi", [P, 4], I32)
            ids_int = own("ids_int", [G, 2, EG], I32)
            ids = own("ids", [G, GS])
            keyi = own("keyi", [P, 4 * G], I32)
            part = own("part", [P, 2, 4 * G], I32)
            hilo = own("hilo", [P, 2, 4, G])
            onehot_hi = own("onehot_hi", [P, 4, HALF], BF16)
            onehot_lo = own("onehot_lo", [P, 4, 2 * P], BF16)
            degree = own("degree", [P, 2, HI])
            degree_T = own("degree_T", [CW, 2, CH, P])
        with ExitStack() as stage:
            own = during(stage)
            group_msg = own("group_msg", [P, 2, 4, ROW])
            keyall = own("keyall", [P, 2, GS])
            same = own("same", [P, 2, 4, GS])
            masked = own("masked", [P, 4, GS])
            repeats = own("repeats", [P, 2, 4])
            todump = own("todump", [P, 2, 4])
            rep_index = own("rep_index", [P, 2, 4], I32)
            summed = own("summed", [P, 2, 4, ROW])
        with ExitStack() as stage:
            own = during(stage)
            h_hi, h_lo = own("h_hi", [P, BLK], F32R), own("h_lo", [P, BLK], F32R)
            a_parts = own("a_parts", [P, BLK], F32R)
            small1 = own("small1", [P, HB, BLK])
            z1 = own("z1", [P, 2, HB, BLK])
            z1_hi, z1_lo = own("z1_hi", [P, 2, HB, BLK], F32R), own("z1_lo", [P, 2, HB, BLK], F32R)
            small2 = own("small2", [P, HB, BLK])
            z2 = own("z2", [P, HB, BLK])

        block = ctx.enter_context(nc.Block())

        s_w = sem("weights_loaded")
        s_bias = sem("mlp_biases_loaded")
        s_pool_const = sem("pool_constants")
        s_pads = sem("ids_pads_written")
        s_ids = sem("ids_loaded")
        s_zeroed = sem("rows_and_columns_zeroed")
        s_idsf = sem("ids_as_floats")
        s_keyrow = sem("keyrow_stored")
        s_keysT = sem("keys_transposed")
        s_keys = sem("keys_ready")
        s_vprep = sem("vector_prelude_steps")
        s_onehot = sem("onehots_written")
        s_count = sem("onehots_counted")
        s_deg = sem("degrees_ready")
        s_degT = sem("degrees_transposed")
        s_degc = sem("degrees_copied")
        s_recip = sem("recip_tables_stored")
        s_ub = sem("u_product_ready")
        s_b1c = sem("bias_columns_ready")
        s_eps = sem("eps_written")
        s_kept, s_src_kept = sem("recips_kept"), sem("src_recips_kept")

        class Dense:
            def __init__(self, n):
                self.load = [sem(f"{n}_rows_loaded{b}") for b in range(4)]
                self.index = sem(f"{n}_index_ready")
                self.gather = [sem(f"{n}_rows_gathered{b}") for b in range(4)]
                if n == "a":
                    self.recip = [sem(f"{n}_recip_gathered{b}") for b in range(4)]
                    self.stats = sem(f"{n}_stats")
                    self.moments = sem(f"{n}_moments")
                    self.spread = sem(f"{n}_spread")
                    self.rstd = sem(f"{n}_rstd")
                    self.normed = sem(f"{n}_normed")
                    self.negmean = sem(f"{n}_end_means_negated")
                    self.centred = sem(f"{n}_end_rows_centred")
                self.T = sem(f"{n}_transposed")
                self.hT = sem(f"{n}_hT_copied")
                self.mm = sem(f"{n}_products")
                self.edge = sem(f"{n}_edge_out_copied")
                self.node = sem(f"{n}_node_out_copied")
                self.store_node = [sem(f"{n}_node_stored{b}") for b in range(4)]
                self.store_edge = [sem(f"{n}_edge_stored{b}") for b in range(4)]

        class Scatter:
            def __init__(self, n):
                self.msg = [sem(f"{n}_messages_loaded{b}") for b in range(2)]
                self.end_index = sem(f"{n}_end_index_ready")
                self.end = [sem(f"{n}_end_rows_gathered{b}") for b in range(2)]
                if n == "d":
                    self.T = sem(f"{n}_end_rows_transposed")
                    self.hT = sem(f"{n}_end_hT_copied")
                    self.end_mm = sem(f"{n}_end_products")
                self.end_msg = sem(f"{n}_src_messages_scaled")
                self.keyall = [sem(f"{n}_keys_loaded{b}") for b in range(2)]
                self.same = sem(f"{n}_same_written")
                if n == "b":
                    self.repeats = sem(f"{n}_repeats_counted")
                    self.todump = sem(f"{n}_way_to_dump")
                    self.moved = sem(f"{n}_offset_chosen")
                self.index = sem(f"{n}_index_ready")
                self.mm = sem(f"{n}_summed_product")
                self.copied = sem(f"{n}_sums_copied")
                self.done = [sem(f"{n}_added{b}") for b in range(2)]

        passed = {nc.scalar.engine: sem("scalar_waits_passed"), nc.vector.engine: sem("vector_waits_passed"), nc.gpsimd.engine: sem("pool_waits_passed")}
        A, C = Dense("a"), Dense("c")
        B, D = Scatter("b"), Scatter("d")
        e_load = [sem(f"e_rows_loaded{b}") for b in range(4)]
        e_x = [sem(f"e_x_added{b}") for b in range(4)]
        e_store = [sem(f"e_out_stored{b}") for b in range(4)]
        e_stats, e_moments, e_spread = sem("e_stats"), sem("e_moments"), sem("e_spread")
        e_rstd, e_normed, e_resid = sem("e_rstd"), sem("e_normed"), sem("e_resid_biased")
        e_T, e_hi, e_ahi, e_lo = sem("e_transposed"), sem("e_h_hi"), sem("e_a_hi"), sem("e_h_and_a_lo")
        e_L1, e_small1, e_z1 = sem("e_L1"), sem("e_small1"), sem("e_z1")
        e_z1hi, e_z1lo = sem("e_z1_hi"), sem("e_z1_lo")
        s_whi, s_split = sem("weights_rounded"), sem("weights_split")
        e_L2, e_small2, e_z2 = sem("e_L2"), sem("e_small2"), sem("e_z2")
        e_L3, e_out = sem("e_L3"), sem("e_out")

        def sweep(eng, n, step):
            step(0)
            with eng.Fori(1, n - 2) as j:
                step(j)
            for j in range(n - 2, n):
                step(j)

        class Step:

            def __init__(self, q, r):
                q, self.b = q + r // 4, r % 4
                self.k, self.turn, self.g, self.half = q * 4 + self.b, q + 1, q * 2 + self.b // 2, self.b % 2
                self.known = isinstance(q, int)
                self.exists = not self.known or 0 <= self.k < STEPS
                self.last = self.known and self.k == STEPS - 1

            def after(self, n):
                return not self.known or self.k >= n

        def ticks(eng, tick, lag):
            for t in range(8):
                tick(lambda n, t=t: Step(0, t - n))
            with eng.Fori(2, STEPS // 4 - 1) as q:
                for t in range(4):
                    tick(lambda n, t=t: Step(q, t - n))
            for t in range(4 + lag):
                tick(lambda n, t=t: Step(STEPS // 4 - 1, t - n))

        def hold(eng):
            eng.sem_inc(passed[eng.engine], 1)

        def before(g, n):
            return not isinstance(g, int) or g >= n

        def block_of(table, st):
            base = N - BLK if st.last else st.k * BLK
            return table[bass.ds(base, BLK), :].rearrange("(p t) f -> p t f", t=T)

        @block.sync
        def _(sp):
            for dst_ap, src_ap in ((W1s[:], W1.rearrange("(c p) f -> p c f", p=P)),
                                   (W2s[:], W2.rearrange("(c p) f -> p c f", p=P)),
                                   (b2s[:], b2.rearrange("(a f) -> a f", a=1).to_broadcast([P, F])),
                                   (w1x[:], w1[0:F, :]), (w1a[0:FA, :], w1[F:ROW, :]), (w1a[FA:P, :], w1[F:ROW, :]),
                                   (w1u[:], w1[ROW:ROW + FA, :]),
                                   (u0[:], u[0:1, :].rearrange("a f -> f a")),
                                   (w2s[:], w2.rearrange("(c p) f -> p c f", p=P)),
                                   (w3s[:], w3.rearrange("(c p) f -> p c f", p=P)),
                                   (b3s[:], b3.rearrange("(a f) -> a f", a=1).to_broadcast([P, F]))):
                sp.dma_start(dst_ap, src_ap).then_inc(s_w, 16)
            sp.wait_ge(s_pads, 1)
            for c, ends in enumerate((dst, src)):
                sp.dma_start(ids_int[0:G - 1, c, :],
                             ends[0:(G - 1) * EG].rearrange("(g e) -> g e", e=EG)).then_inc(s_ids, 16)
                sp.dma_start(ids_int[G - 1:G, c, 0:TAIL],
                             ends[(G - 1) * EG:E].rearrange("(g e) -> g e", g=1)).then_inc(s_ids, 16)
            for col, vec in ((bias1, b1m), (bias2, b2m), (b1col, b1)):
                sp.dma_start(col[:], vec.rearrange("(m p) -> p m", p=P), allow_slow_non_contiguous=True).then_inc(s_bias, 16)
            sp.wait_ge(s_idsf, 1)
            sp.dma_start(keyrow, ids[:]).then_inc(s_keyrow, 16)
            sp.wait_ge(s_pool_const, 1)
            for table in (pre1, node1):
                sp.dma_start(table[N:NR, 0:F].rearrange("(p r) f -> p r f", r=8),
                             zeros[0:(NR - N) // 8, :].rearrange("p (r f) -> p r f", f=F)).then_inc(s_zeroed, 16)
            columns = node1[:, F:ROW].rearrange("(p c r) f -> c p r f", p=P, c=4)
            for c in range(4):
                sp.dma_start(columns[c], zeros[:, 0:FA].unsqueeze(1).to_broadcast([P, NR // P // 4, FA]))\
                    .then_inc(s_zeroed, 16)
            for c, table in enumerate((recip_in, recip_out)):
                sp.wait_ge(s_degc, c + 1)
                sp.dma_start(table.rearrange("(q r) a -> q (r a)", q=CW),
                             degree_T[:, c].rearrange("p c f -> p (c f)")).then_inc(s_recip, 16)

            def dense(S, source, target):
                def load(st):
                    if st.after(4):
                        sp.wait_ge(S.normed if S is A else S.T, st.k - 3)
                    sp.dma_start(rows[:, st.b, 0:T, :], block_of(source, st)).then_inc(S.load[st.b], 16)

                def tick(at):
                    st = at(3)
                    if st.exists:
                        sp.wait_ge(S.node, st.k + 1)
                        if st.last:
                            sp.wait_ge(S.store_node[st.b - 1], 16 * st.turn)
                        sp.dma_start(block_of(target, st)[:, :, 0:F], node_out[:, st.b, :, 0:F]).then_inc(S.store_node[st.b], 16)
                        sp.wait_ge(S.edge, st.k + 1)
                        if S is A:
                            sp.dma_start(msg1[bass.ds(st.g, 1), :, st.half::2, :].rearrange("g p s f -> (g p) s f"),
                                         edge_out[:, st.b]).then_inc(S.store_edge[st.b], 16)
                        else:
                            sp.dma_start(msg2[bass.ds(st.g, 1), :, st.half, :].rearrange("g p f -> (g p) f"),
                                         edge_out[:, st.b, 0, :]).then_inc(S.store_edge[st.b], 16)
                    st = at(-3)
                    if st.exists:
                        load(st)
                for k in range(3):
                    load(Step(0, k))
                ticks(sp, tick, 3)

            def scatter(S, X, msg, with_attr):
                if not with_attr:
                    sp.wait_ge(s_keyrow, 16)
                    sp.wait_ge(s_zeroed, 16 * 6)

                def step(g, b, uses):
                    if before(g, 2):
                        sp.wait_ge(S.mm, g - 1)
                    sp.dma_start(keyall[:, b, :], keyrow[bass.ds(g, 1), :].to_broadcast([P, GS])).then_inc(S.keyall[b], 16)
                    if isinstance(g, int) and g == 0:
                        for q in range(4):
                            sp.wait_ge(X.store_edge[q], 16 * STEPS // 4)
                    one = msg[bass.ds(g, 1)].rearrange("g p s f -> (g p) s f")
                    sp.dma_start(group_msg[:, b, 0:one.shape[1], 0:F], one).then_inc(S.msg[b], 16)
                    if with_attr:
                        if isinstance(g, int) and g == G - 1:
                            sp.dma_start(group_msg[:, b, 0, F:ROW], edge_attr[g * EG:g * EG + P, :]).then_inc(S.msg[b], 16)
                            sp.dma_start(group_msg[0:TAIL - P, b, 1, F:ROW], edge_attr[g * EG + P:E, :]).then_inc(S.msg[b], 16)
                        else:
                            for s in range(2):
                                sp.dma_start(group_msg[:, b, s, F:ROW], edge_attr[bass.ds(g * EG + s * P, P), :])\
                                    .then_inc(S.msg[b], 16)

                sweep(sp, G // 2, lambda j: [step(j * 2 + b, b, j + 1) for b in range(2)])

            dense(A, x, pre1)
            scatter(B, A, msg1, False)
            for b in range(2):
                sp.wait_ge(B.done[b], 64 * G // 2)
            dense(C, pre1, node1)
            scatter(D, C, msg2, True)
            for b in range(2):
                sp.wait_ge(D.done[b], 64 * G // 2)

            def load(st):
                if st.after(4):
                    sp.wait_ge(e_T, st.k - 3)
                    sp.wait_ge(e_resid, st.k - 3)
                rows1 = block_of(node1, st)
                sp.dma_start(node_out[:, st.b, :, 0:ROW], rows1).then_inc(e_load[st.b], 16)
                sp.dma_start(node_out[:, st.b, :, ROW:F + P], rows1[:, :, F:ROW]).then_inc(e_load[st.b], 16)
            for k in range(2):
                load(Step(0, k))

            def tick(at):
                st = at(-2)
                if st.exists:
                    load(st)
                st = at(4)
                if st.exists:
                    sp.wait_ge(e_out, st.k + 1)
                    if st.last:
                        sp.wait_ge(e_store[st.b - 1], 16 * st.turn)
                    sp.dma_start(block_of(out, st), rows[:, st.b, 0:T, :]).then_inc(e_store[st.b], 16)
            ticks(sp, tick, 4)
            for b in range(4):
                sp.wait_ge(e_store[b], 16 * STEPS // 4)

        @block.gpsimd
        def _(pool):
            pool.memset(zeros[:], 0.0).then_inc(s_pool_const, 1)
            pool.iota(ids_int[:], pattern=[[0, 2], [1, EG]], base=N, channel_multiplier=0).then_inc(s_pads, 1)
            pool.memset(ident[:], 0.0).then_inc(s_pool_const, 1)
            pool.memset(later[:], 1.0).then_inc(s_pool_const, 1)
            pool.iota(iota_hi[:], pattern=[[1, HALF]], base=0, channel_multiplier=0,
                      allow_small_or_imprecise_dtypes=True).then_inc(s_pool_const, 1)
            pool.iota(iota_lo[:], pattern=[[1, 2 * P]], base=0, channel_multiplier=0,
                      allow_small_or_imprecise_dtypes=True).then_inc(s_pool_const, 1)
            pool.iota(dumpi[:], pattern=[[P, 4]], base=DUMP, channel_multiplier=1).then_inc(s_pool_const, 1)
            pool.wait_ge(s_pool_const, 6)
            pool.affine_select(out=ident[:], in_=ident[:], compare_op=ALU.not_equal, fill=1.0, base=0,
                               pattern=[[-1, P]], channel_multiplier=1).then_inc(s_pool_const, 1)
            pool.affine_select(out=later[:], in_=later[:], compare_op=ALU.is_gt, fill=0.0, base=0,
                               pattern=[[1, GS]], channel_multiplier=-1).then_inc(s_pool_const, 1)
            pool.tensor_copy(dumpcol[:], dumpi[:]).then_inc(s_pool_const, 1)

            def gather(S, st, table):
                b = st.b
                if st.after(4):
                    pool.wait_ge(S.centred if S is A else S.T, st.k - 3)
                pool.wait_ge(S.index, st.k + 1)
                hold(pool)
                for slot, col in ((T, 1), (T + 1, 0))[0:2 if S is A else 1]:
                    pool.indirect_dma_start(rows[:, b, slot, :], None, table,
                                            bass.IndirectOffsetOnAxis(ap=index[:, b, col:col + 1], axis=0))\
                        .then_inc(S.gather[b], 16)

            def gather_recip(st):
                if st.after(4):
                    pool.wait_ge(s_kept, st.k - 3)
                    hold(pool)
                pool.indirect_dma_start(recip_buf[:, st.b, 0:1], None, recip_in,
                                        bass.IndirectOffsetOnAxis(ap=index[:, st.b, 2:3], axis=0))\
                    .then_inc(A.recip[st.b], 16)

            def ends(S, g, b):
                pool.wait_ge(S.end_index, g + 1)
                hold(pool)
                for s in range(2):
                    to = recip_buf[:, b, s:s + 1] if S is B else rows[:, b, s, :]
                    pool.indirect_dma_start(to, None, recip_out if S is B else pre1,
                                            bass.IndirectOffsetOnAxis(ap=index[:, b, s:s + 1], axis=0))\
                        .then_inc(S.end[b], 16)

            def scatter(S, X, target, width):
                for g in range(2):
                    ends(S, g, g)
                for b in range(4):
                    pool.wait_ge(X.store_node[b], 16 * STEPS // 4)
                pool.wait_ge(s_zeroed, 16 * 6)

                def step(g, b, uses):
                    if not isinstance(g, int) or g + 2 < G:
                        pool.wait_ge(S.end_msg if S is B else S.T, g + 1)
                        ends(S, g + 2, b)
                    pool.wait_ge(S.copied, g + 1)
                    pool.wait_ge(S.index, g + 1)
                    if before(g, 1):
                        last = (uses - 1) if b == 0 else uses
                        pool.wait_ge(S.done[1 - b], last * 64)
                    hold(pool)
                    for s in range(4):
                        pool.indirect_dma_start(target, bass.IndirectOffsetOnAxis(ap=rep_index[:, b, s:s + 1], axis=0),
                                                summed[:, b, s, 0:width], None, compute_op=ALU.add).then_inc(S.done[b], 16)

                sweep(pool, G // 2, lambda j: [step(j * 2 + b, b, j + 1) for b in range(2)])

            for k in range(3):
                gather(A, Step(0, k), x)
            pool.wait_ge(s_recip, 32)
            for k in range(2):
                gather_recip(Step(0, k))

            def tick(at):
                st = at(-2)
                if st.exists:
                    gather_recip(st)
                st = at(-3)
                if st.exists:
                    gather(A, st, x)
            ticks(pool, tick, 0)
            pool.wait_ge(s_kept, STEPS)
            scatter(B, A, pre1, F)
            for b in range(2):
                pool.wait_ge(B.done[b], 64 * G // 2)
            ticks(pool, lambda at: gather(C, at(0), pre1), 0)
            pool.wait_ge(C.T, STEPS)
            scatter(D, C, node1, ROW)

            def add_x(st):
                pool.wait_ge(e_load[st.b], 32 * st.turn)
                pool.dma_start(node_out[:, st.b, :, 0:F], block_of(x, st), accum_op=ALU.add).then_inc(e_x[st.b], 16)
            add_x(Step(0, 0))

            def tick(at):
                st = at(-1)
                if st.exists:
                    add_x(st)
                st = at(0)
                if st.exists:
                    b = st.b
                    pool.wait_ge(e_x[b], 16 * st.turn)
                    if st.after(4):
                        pool.wait_ge(e_out, st.k - 3)
                    for s in range(T):
                        last = pool.tensor_tensor(resid[:, b, s, :], node_out[:, b, s, 0:F], b3s[:], ALU.add)
                    last.then_inc(e_resid, 1)
                st = at(2)
                if st.exists:
                    for m in range(HB):
                        pool.wait_ge(e_z1hi, st.k * HB + (m + 1))
                        if st.after(2):
                            pool.wait_ge(e_L2, st.k * HB + (HB - 2 * HB))
                        pool.tensor_tensor(z1_lo[:, st.b % 2, m, :], z1[:, st.b % 2, m, :], z1_hi[:, st.b % 2, m, :].bitcast(F32),
                                           ALU.subtract).then_inc(e_z1lo, 1)
            ticks(pool, tick, 2)

        @block.scalar
        def _(act):
            act.wait_ge(s_keys, 1)

            def stage_index(S, st):
                if st.after(4):
                    act.wait_ge(S.gather[st.b], (32 if S is A else 16) * (st.turn - 1))
                    if S is A:
                        act.wait_ge(S.recip[st.b], 16 * (st.turn - 1))
                act.activation(index[:, st.b, :].rearrange("p (a s) -> p a s", a=2),
                               keys[:, :, st.half::2, bass.ds(st.g, 1)].rearrange("p a s g -> p a (s g)"),
                               ACT.Copy).then_inc(S.index, 1)

            def copy_hT(S, st):
                bias = b1col[:, 0:1] if S is C else 0.0
                act.wait_ge(S.T, st.k + 1)
                o = 2 * (st.b % 2)
                act.activation(hT[:, st.b, 0:4, :].rearrange("p s f -> p (s f)"), bank[o][:], ACT.Relu, bias=bias)
                e = 2 if S is A else 1
                act.activation(hT[:, st.b, T:T + e, :].rearrange("p s f -> p (s f)"), bank[o + 1][:, 0:e * P], ACT.Relu,
                               bias=bias).then_inc(S.hT, 1)

            def copy_edge(S, st):
                if st.after(4):
                    act.wait_ge(S.store_edge[st.b], 16 * (st.turn - 1))
                    hold(act)
                products = bank[5 + 2 * (st.b % 2)]
                last = act.activation(edge_out[:, st.b, 0, :], products[:, 0:P], ACT.Copy,
                                      scale=endscale[:, st.b:st.b + 1] if S is A else recip[:, st.half, bass.ds(st.g, 1)])
                if S is A:
                    last = act.activation(edge_out[:, st.b, 1, :], products[:, P:2 * P], ACT.Copy,
                                          scale=rstd[:, st.b, T + 1:T + 2])
                last.then_inc(S.edge, 1)

            act.wait_ge(s_eps, 1)
            for k in range(3):
                stage_index(A, Step(0, k))

            def tick(at):
                st = at(1)
                if st.exists:
                    act.wait_ge(A.negmean, st.k + 1)
                    if st.after(4):
                        act.wait_ge(A.T, st.k - 3)
                    for s in range(2):
                        last = act.activation(normed[:, st.b, T + s, :], rows[:, st.b, T + s, :], ACT.Identity,
                                              bias=negmean[:, st.b, s:s + 1])
                    last.then_inc(A.centred, 1)
                    act.wait_ge(A.recip[st.b], 16 * st.turn)
                    act.activation(recip[:, st.half, bass.ds(st.g, 1)], recip_buf[:, st.b, 0:1], ACT.Copy)
                    act.wait_ge(A.rstd, st.k + 1)
                    act.activation(endscale[:, st.b:st.b + 1], recip_buf[:, st.b, 0:1], ACT.Copy,
                                   scale=rstd[:, st.b, T:T + 1]).then_inc(s_kept, 1)
                st = at(3)
                if st.exists:
                    act.wait_ge(A.mm, st.k + 1)
                    if st.after(4):
                        act.wait_ge(A.store_node[st.b], 16 * (st.turn - 1))
                    act.activation(node_out[:, st.b, :, 0:F], bank[4 + 2 * (st.b % 2)][:].rearrange("p (t f) -> p t f", t=T),
                                   ACT.Copy).then_inc(A.node, 1)
                    act.wait_ge(s_kept, st.k + 1)
                    copy_edge(A, st)
                st = at(0)
                if st.exists:
                    act.wait_ge(A.moments, st.k + 1)
                    act.activation(spread[:, st.b, :], moments[:, st.b, :, 1], ACT.Sqrt, bias=eps[:, 0:1]).then_inc(A.spread, 1)
                st = at(-3)
                if st.exists:
                    stage_index(A, st)
                st = at(1)
                if st.exists:
                    copy_hT(A, st)
            ticks(act, tick, 3)

            def end_index(S, g, b):
                act.activation(index[:, b, 0:2], (keys[:, 1, 2:4, bass.ds(g, 1)] if S is B else
                                                  keys[:, 0, 0:2, bass.ds(g, 1)]).rearrange("p s g -> p (s g)"),
                               ACT.Copy).then_inc(S.end_index, 1)

            def end_rows(S, g, b, uses):
                act.wait_ge(S.end[b], 32 * uses)
                if S is D:
                    act.wait_ge(S.T, g + 1)
                    act.activation(hT[:, b, 0:2, :].rearrange("p s f -> p (s f)"), bank[b][:, 0:2 * P], ACT.Relu,
                                   bias=b1col[:, 0:1]).then_inc(S.hT, 1)
                if not isinstance(g, int) or g + 2 < G:
                    hold(act)
                    end_index(S, g + 2, b)

            def end_messages(S, g, b, uses):
                if S is B:
                    act.activation(recip[:, 2:4, bass.ds(g, 1)].rearrange("p s g -> p (s g)"), recip_buf[:, b, :],
                                   ACT.Copy).then_inc(s_src_kept, 1)
                    act.wait_ge(S.msg[b], 16 * uses)
                    for s in range(2):
                        last = act.activation(group_msg[:, b, 2 + s, 0:F], group_msg[:, b, 2 + s, 0:F], ACT.Copy,
                                              scale=recip_buf[:, b, s:s + 1])
                else:
                    act.wait_ge(S.end_mm, g + 1)
                    if before(g, 2):
                        act.wait_ge(S.mm, g - 1)
                    hold(act)
                    for s in range(2):
                        last = act.activation(group_msg[:, b, 2 + s, 0:F], bank[2 + b][:, s * P:(s + 1) * P], ACT.Copy,
                                              scale=recip[:, 2 + s, bass.ds(g, 1)])
                last.then_inc(S.end_msg, 1)

            def scatter(S):
                for g in range(2):
                    end_index(S, g, g)
                end_rows(S, 0, 0, 1)
                end_messages(S, 0, 0, 1)

                def step(g, b, uses):
                    if S is B:
                        act.wait_ge(S.mm, g + 1)
                        if before(g, 2):
                            act.wait_ge(S.done[b], 64 * (uses - 1))
                        for c in range(2):
                            last = act.activation(summed[:, b, 2 * c:2 * c + 2, 0:F],
                                                  bank[4 + 2 * b + c][:].rearrange("p (s f) -> p s f", s=2)[:, :, 0:F],
                                                  ACT.Copy)
                        last.then_inc(S.copied, 1)
                    if not isinstance(g, int) or g + 1 < G:
                        end_rows(S, g + 1, 1 - b, uses + b)
                        end_messages(S, g + 1, 1 - b, uses + b)
                sweep(act, G // 2, lambda j: [step(j * 2 + b, b, j + 1) for b in range(2)])

            scatter(B)

            for k in range(3):
                stage_index(C, Step(0, k))

            def tick(at):
                st = at(-3)
                if st.exists:
                    stage_index(C, st)
                st = at(1)
                if st.exists:
                    copy_hT(C, st)
                st = at(2)
                if st.exists:
                    act.wait_ge(C.mm, st.k + 1)
                    copy_edge(C, st)
            act.wait_ge(s_kept, STEPS)
            act.wait_ge(s_src_kept, G)
            ticks(act, tick, 2)
            scatter(D)

            act.wait_ge(s_b1c, 4)

            def scaled(st, products, first_bank, bias_small, small, ready):
                for m in range(HB):
                    act.wait_ge(products, st.k * HB + (m + 1))
                    act.activation(small[:, m, :], bank[first_bank + m][:], ACT.Identity, scale=SLOPE,
                                   bias=bias_small[:, m:m + 1]).then_inc(ready, 1)

            def tick(at):
                st = at(4)
                if st.exists:
                    scaled(st, e_L2, 2, bias2_small, small2, e_small2)
                st = at(2)
                if st.exists:
                    scaled(st, e_L1, 0, bias1_small, small1, e_small1)
                st = at(1)
                if st.exists:
                    act.wait_ge(e_T, st.k + 1)
                    act.activation(h_hi[:], bank[5][:], ACT.Relu).then_inc(e_hi, 1)
                    act.activation(a_parts[:], bank[6][:], ACT.Copy).then_inc(e_ahi, 1)
                st = at(2)
                if st.exists:
                    for m in range(HB):
                        act.wait_ge(e_z1, st.k * HB + (m + 1))
                        if st.after(2):
                            act.wait_ge(e_L2, st.k * HB + (HB - 2 * HB))
                        act.activation(z1_hi[:, st.b % 2, m, :], z1[:, st.b % 2, m, :], ACT.Copy).then_inc(e_z1hi, 1)
                st = at(0)
                if st.exists:
                    act.wait_ge(e_moments, st.k + 1)
                    act.activation(spread[:, st.b, 0:T], moments[:, st.b, 0:T, 1], ACT.Sqrt, bias=eps[:, 0:1])\
                        .then_inc(e_spread, 1)
            ticks(act, tick, 4)

        @block.vector
        def _(dve):
            dve.memset(eps[:], EPS).then_inc(s_eps, 1)
            dve.wait_ge(s_ids, 64)
            dve.tensor_copy(ids[:], ids_int[:].rearrange("g c e -> g (c e)")).then_inc(s_idsf, 1)
            kk = keys[:, 1].rearrange("p s g -> p (s g)")
            dve.wait_ge(s_keysT, 1)
            dve.tensor_copy(kk, bank[0][:, 0:4 * G]).then_inc(s_vprep, 1)
            dve.wait_ge(s_vprep, 1)
            dve.tensor_scalar(keys[:, 0].rearrange("p s g -> p (s g)"), kk, float(N - 1), None, ALU.min).then_inc(s_keys, 1)
            dve.tensor_copy(keyi[:], kk).then_inc(s_vprep, 1)
            dve.wait_ge(s_vprep, 2)
            dve.tensor_scalar(part[:, 0], keyi[:], 8, None, ALU.logical_shift_right).then_inc(s_vprep, 1)
            dve.tensor_scalar(part[:, 1], keyi[:], 2 * P - 1, None, ALU.bitwise_and).then_inc(s_vprep, 1)
            dve.wait_ge(s_vprep, 4)
            dve.tensor_copy(hilo[:].rearrange("p a s g -> p a (s g)"), part[:]).then_inc(s_vprep, 1)
            dve.wait_ge(s_vprep, 5)
            dve.wait_ge(s_pool_const, 9)

            def onehots(g):
                for s in range(4):
                    if before(g, 1):
                        dve.wait_ge(s_count, g * 4 + s - 3)
                    dve.tensor_scalar(onehot_lo[:, s, :], iota_lo[:], hilo[:, 1, s, bass.ds(g, 1)], None, ALU.is_equal)
                    dve.tensor_scalar(onehot_hi[:, s, :], iota_hi[:], hilo[:, 0, s, bass.ds(g, 1)], None, ALU.is_equal)\
                        .then_inc(s_onehot, 1)
            sweep(dve, G // 2, lambda j: [onehots(j * 2 + b) for b in range(2)])
            dve.wait_ge(s_count, 4 * G)
            for c in range(2):
                blocks = degree[:, c].rearrange("p (h l) -> p l h", l=2)
                for h in range(2):
                    last = dve.tensor_scalar(blocks[:, h, :], bank[2 * c + h][:, 0:HALF], 1.0, None, ALU.max)
                last.then_inc(s_vprep, 1)
                dve.wait_ge(s_vprep, 6 + c)
                dve.reciprocal(degree[:, c], degree[:, c]).then_inc(s_deg, 1)
            for c in range(2):
                dve.wait_ge(s_degT, c + 1)
                dve.tensor_copy(degree_T[:, c, 0:4, :], bank[4 + 2 * c][0:CW, :].rearrange("p (c f) -> p c f", f=P))
                dve.tensor_copy(degree_T[:, c, 4:CH, :], bank[5 + 2 * c][0:CW, 0:(CH - 4) * P].rearrange("p (c f) -> p c f", f=P))\
                    .then_inc(s_degc, 1)
            dve.wait_ge(s_w, 16 * 11)
            pairs = ((w1x, w1x_hi, w1x_lo), (w1a, w1a_hi, w1a_lo), (w2s, w2_hi, w2_lo))
            for w, hi, _ in pairs:
                dve.tensor_copy(hi[:], w[:]).then_inc(s_whi, 1)
            dve.wait_ge(s_whi, len(pairs))
            for w, hi, lo in pairs:
                dve.tensor_tensor(lo[:], w[:], hi[:].bitcast(F32), ALU.subtract).then_inc(s_split, 1)
            dve.wait_ge(s_ub, 1)
            dve.wait_ge(s_bias, 48)
            dve.tensor_tensor(bias1[:], bank[0][:, 0:HB], bias1[:], ALU.add).then_inc(s_b1c, 1)
            dve.wait_ge(s_b1c, 1)
            dve.tensor_scalar(bias1_small[:], bias1[:], SLOPE, None, ALU.mult).then_inc(s_b1c, 1)
            dve.tensor_scalar(bias2_small[:], bias2[:], SLOPE, None, ALU.mult).then_inc(s_b1c, 2)

            def stats_of(st, s_stats, n, source):
                for s in range(n):
                    last = dve.bn_stats(stats[:, st.b, s, :], source(st.b, s))
                last.then_inc(s_stats, 1)

            def moments_of(st, s_stats, s_moments, n):
                dve.wait_ge(s_stats, st.k + 1)
                hold(dve)
                for s in range(n):
                    last = dve.bn_aggr(moments[:, st.b, s, :], stats[:, st.b, s, :])
                last.then_inc(s_moments, 1)

            def rstd_of(st, s_spread, s_rstd, n):
                dve.wait_ge(s_spread, st.k + 1)
                dve.reciprocal(rstd[:, st.b, 0:n], spread[:, st.b, 0:n]).then_inc(s_rstd, 1)

            def normalise(st, s_rstd, s_normed, s_read, n, source):
                if st.after(4):
                    dve.wait_ge(s_read, st.k - 3)
                dve.wait_ge(s_rstd, st.k + 1)
                for s in range(n):
                    last = dve.tensor_scalar(normed[:, st.b, s, :], source(st.b, s), moments[:, st.b, s, 0:1],
                                             rstd[:, st.b, s:s + 1], ALU.subtract, ALU.mult)
                last.then_inc(s_normed, 1)

            def tick(at):
                st, previous = at(0), at(1)
                if st.exists:
                    dve.wait_ge(A.load[st.b], 16 * st.turn)
                    dve.wait_ge(A.gather[st.b], 32 * st.turn)
                    stats_of(st, A.stats, 6, lambda b, s: rows[:, b, s, :])
                if previous.exists:
                    rstd_of(previous, A.spread, A.rstd, 6)
                    dve.wait_ge(A.moments, previous.k + 1)
                    if previous.after(4):
                        dve.wait_ge(A.centred, previous.k - 3)
                    dve.tensor_scalar(negmean[:, previous.b, :], moments[:, previous.b, T:T + 2, 0], -1.0, None, ALU.mult)\
                        .then_inc(A.negmean, 1)
                if st.exists:
                    moments_of(st, A.stats, A.moments, 6)
                if previous.exists:
                    normalise(previous, A.rstd, A.normed, A.T, T, lambda b, s: rows[:, b, s, :])
            ticks(dve, tick, 1)

            def same_keys(S, g, b, uses):
                dve.wait_ge(S.keyall[b], 16 * uses)
                if before(g, 2):
                    dve.wait_ge(S.mm, g - 1)
                for s in range(4):
                    last = dve.tensor_scalar(same[:, b, s, s * P:GS], keyall[:, b, s * P:GS],
                                             keys[:, 1, s, bass.ds(g, 1)], None, ALU.is_equal)
                last.then_inc(S.same, 1)

            def scatter_B(S):
                def step(g, b, uses):
                    same_keys(S, g, b, uses)
                    dve.wait_ge(S.same, g + 1)
                    for s in range(4):
                        last = dve.tensor_tensor_reduce(masked[:, s, s * P:GS], same[:, b, s, s * P:GS], later[:, 0:GS - s * P],
                                                        1.0, 0.0, ALU.mult, ALU.add, repeats[:, b, s:s + 1])
                    dve.tensor_tensor(todump[:, b, :], dumpcol[:], keys[:, 1, :, bass.ds(g, 1)].rearrange("p s g -> p (s g)"),
                                      ALU.subtract).then_inc(S.todump, 1)
                    dve.wait_ge(S.todump, g + 1)
                    dve.scalar_tensor_tensor(out=todump[:, b, :], in0=repeats[:, b, :], scalar=0.0, in1=todump[:, b, :],
                                             op0=ALU.is_gt, op1=ALU.mult).then_inc(S.moved, 1)
                    dve.wait_ge(S.moved, g + 1)
                    rk = repkey[:, :, bass.ds(g, 1)].rearrange("p s g -> p (s g)")
                    dve.tensor_tensor(rk, keys[:, 1, :, bass.ds(g, 1)].rearrange("p s g -> p (s g)"), todump[:, b, :], ALU.add)\
                        .then_inc(S.repeats, 1)
                    if before(g, 2):
                        dve.wait_ge(S.done[b], 64 * (uses - 1))
                    dve.wait_ge(S.repeats, g + 1)
                    dve.tensor_scalar(rep_index[:, b, :], rk, 0.0, None, ALU.add).then_inc(S.index, 1)
                sweep(dve, G // 2, lambda j: [step(j * 2 + b, b, j + 1) for b in range(2)])
            scatter_B(B)

            def tick(at):
                st = at(2)
                if st.exists:
                    dve.wait_ge(C.mm, st.k + 1)
                    if st.after(4):
                        dve.wait_ge(C.store_node[st.b], 16 * (st.turn - 1))
                    dve.tensor_tensor(node_out[:, st.b, :, 0:F], bank[4 + 2 * (st.b % 2)][:].rearrange("p (t f) -> p t f", t=T),
                                      b2s[:].unsqueeze(1).to_broadcast([P, T, F]), ALU.add).then_inc(C.node, 1)
            ticks(dve, tick, 2)
            same_keys(D, 0, 0, 1)

            def step(g, b, uses):
                if not isinstance(g, int) or g + 1 < G:
                    same_keys(D, g + 1, 1 - b, uses + b)
                dve.wait_ge(D.mm, g + 1)
                if before(g, 2):
                    dve.wait_ge(D.done[b], 64 * (uses - 1))
                dve.tensor_scalar(rep_index[:, b, :], repkey[:, :, bass.ds(g, 1)].rearrange("p s g -> p (s g)"), 0.0, None,
                                  ALU.add).then_inc(D.index, 1)
                for c in range(2):
                    last = dve.tensor_copy(summed[:, b, 2 * c:2 * c + 2, :],
                                           bank[4 + 2 * b + c][:].rearrange("p (s f) -> p s f", s=2)[:, :, 0:ROW])
                last.then_inc(D.copied, 1)
            sweep(dve, G // 2, lambda j: [step(j * 2 + b, b, j + 1) for b in range(2)])

            def leaky(st, small_ready, first_bank, bias, small, z, ready):
                for m in range(HB):
                    dve.wait_ge(small_ready, st.k * HB + (m + 1))
                    dve.scalar_tensor_tensor(out=z[:, m, :], in0=bank[first_bank + m][:], scalar=bias[:, m:m + 1],
                                             in1=small[:, m, :], op0=ALU.add, op1=ALU.max).then_inc(ready, 1)

            def tick(at):
                st = at(1)
                if st.exists:
                    rstd_of(st, e_spread, e_rstd, T)
                    normalise(st, e_rstd, e_normed, e_T, T, lambda b, s: node_out[:, b, s, 0:F])
                st = at(4)
                if st.exists:
                    leaky(st, e_small2, 2, bias2, small2, z2, e_z2)
                st = at(2)
                if st.exists:
                    if st.after(2):
                        dve.wait_ge(e_z1lo, st.k * HB - HB)
                    leaky(st, e_small1, 0, bias1, small1, z1[:, st.b % 2], e_z1)
                st = at(1)
                if st.exists:
                    dve.wait_ge(e_hi, st.k + 1)
                    dve.scalar_tensor_tensor(out=h_lo[:], in0=bank[5][:], scalar=0.0, in1=h_hi[:].bitcast(F32),
                                             op0=ALU.max, op1=ALU.subtract)
                    dve.wait_ge(e_ahi, st.k + 1)
                    dve.tensor_tensor(a_parts[FA:P, :], bank[6][FA:P, :], a_parts[FA:P, :].bitcast(F32), ALU.subtract)\
                        .then_inc(e_lo, 1)
                st = at(0)
                if st.exists:
                    dve.wait_ge(e_x[st.b], 16 * st.turn)
                    stats_of(st, e_stats, T, lambda b, s: node_out[:, b, s, 0:F])
                    moments_of(st, e_stats, e_moments, T)
                st = at(4)
                if st.exists:
                    dve.wait_ge(e_L3, st.k + 1)
                    dve.wait_ge(e_resid, st.k + 1)
                    if st.after(4):
                        dve.wait_ge(e_store[st.b], 16 * (st.turn - 1))
                    dve.tensor_tensor(rows[:, st.b, 0:T, :], bank[4][:].rearrange("p (t f) -> p t f", t=T),
                                      resid[:, st.b], ALU.add).then_inc(e_out, 1)
            ticks(dve, tick, 4)

        @block.tensor
        def _(pe):
            pe.wait_ge(s_pool_const, 9)
            pe.wait_ge(s_idsf, 1)
            for s in range(4):
                last = pe.transpose(bank[0][:, s * G:(s + 1) * G], ids[:, s * P:(s + 1) * P], ident[0:G, 0:G])
            last.then_inc(s_keysT, 1)
            pe.wait_ge(s_keys, 1)

            def count(g):
                for s in range(4):
                    pe.wait_ge(s_onehot, g * 4 + s + 1)
                    for h in range(2):
                        last = pe.matmul(bank[2 * (s // 2) + h][:, 0:HALF], onehot_lo[:, s, h * P:(h + 1) * P],
                                         onehot_hi[:, s, :],
                                         start=(isinstance(g, int) and g == 0 and s % 2 == 0),
                                         stop=(isinstance(g, int) and g == G - 1 and s % 2 == 1))
                    last.then_inc(s_count, 1)
            sweep(pe, G // 2, lambda j: [count(j * 2 + b) for b in range(2)])
            for c in range(2):
                pe.wait_ge(s_deg, c + 1)
                cols = degree[:, c].rearrange("p (q r) -> p r q", r=CH)
                for r in range(CH):
                    last = pe.transpose(bank[4 + 2 * c + r // 4][0:CW, (r % 4) * P:(r % 4 + 1) * P], cols[:, r, :], ident[:])
                last.then_inc(s_degT, 1)
            pe.wait_ge(s_w, 16 * 11)
            for m in range(HB):
                last = pe.matmul(bank[0][:, m:m + 1], w1u[:, m * P:(m + 1) * P], u0[:], start=True, stop=True)
            last.then_inc(s_ub, 1)

            def dense_transposes(S, st, source, ready):
                ready(st)
                if st.after(2):
                    pe.wait_ge(S.hT, st.k - 1)
                for s in range(T + (2 if S is A else 1)):
                    last = pe.transpose(bank[s // 4 + 2 * (st.b % 2)][:, (s % 4) * P:(s % 4 + 1) * P],
                                        source[:, st.b, s, :], ident[:])
                last.then_inc(S.T, 1)

            def dense_products(S, st, W):
                pe.wait_ge(S.hT, st.k + 1)
                if st.after(2):
                    pe.wait_ge(S.node, st.k - 1)
                    pe.wait_ge(S.edge, st.k - 1)
                for s in range(T):
                    o = bank[4 + 2 * (st.b % 2)][:, s * P:(s + 1) * P]
                    pe.matmul(o, hT[:, st.b, s, :], W[:, 0, :], start=True, stop=True)
                for s in range(2 if S is A else 1):
                    last = pe.matmul(bank[5 + 2 * (st.b % 2)][:, s * P:(s + 1) * P], hT[:, st.b, T + s, :],
                                     W[:, 1 + s, :], start=True, stop=True)
                last.then_inc(S.mm, 1)

            def scatter(S, with_attr):
                def end_transposes(g, b, uses):
                    pe.wait_ge(S.end[b], 32 * uses)
                    if before(g, 2):
                        pe.wait_ge(S.hT, g - 1)
                    for s in range(2):
                        last = pe.transpose(bank[b][:, s * P:(s + 1) * P], rows[:, b, s, :], ident[:])
                    last.then_inc(S.T, 1)

                def end_products(g, b):
                    pe.wait_ge(S.hT, g + 1)
                    if before(g, 2):
                        pe.wait_ge(S.end_msg, g - 1)
                    for s in range(2):
                        last = pe.matmul(bank[2 + b][:, s * P:(s + 1) * P], hT[:, b, s, :], W2s[:, 2, :],
                                         start=True, stop=True)
                    last.then_inc(S.end_mm, 1)

                if with_attr:
                    end_transposes(0, 0, 1)
                    end_products(0, 0)

                def step(g, b, uses):
                    follows = with_attr and (not isinstance(g, int) or g + 1 < G)
                    pe.wait_ge(S.same, g + 1)
                    pe.wait_ge(S.msg[b], (48 if with_attr else 16) * uses)
                    pe.wait_ge(S.end_msg, g + 1)
                    if before(g, 2):
                        pe.wait_ge(S.copied, g - 1)
                    for i in range(4):
                        if follows and i == 3:
                            end_transposes(g + 1, 1 - b, uses + b)
                        for j in range(i + 1):
                            w = ROW if with_attr and j < 2 else F
                            o = bank[4 + 2 * b + i // 2][:, (i % 2) * 256:(i % 2) * 256 + w]
                            last = pe.matmul(o, same[:, b, j, i * P:(i + 1) * P], group_msg[:, b, j, 0:w],
                                             start=(j == 0), stop=(j == i))
                    last.then_inc(S.mm, 1)
                    if follows:
                        end_products(g + 1, 1 - b)
                sweep(pe, G // 2, lambda j: [step(j * 2 + b, b, j + 1) for b in range(2)])

            def a_ready(st):
                pe.wait_ge(A.normed, st.k + 1)
                pe.wait_ge(A.centred, st.k + 1)
            pe.wait_ge(s_degc, 2)
            pe.wait_ge(s_b1c, 1)

            def tick(at):
                if at(2).exists:
                    dense_products(A, at(2), W1s)
                if at(1).exists:
                    dense_transposes(A, at(1), normed, a_ready)
            ticks(pe, tick, 2)
            pe.wait_ge(A.edge, STEPS)
            scatter(B, False)

            def c_ready(st):
                pe.wait_ge(C.load[st.b], 16 * st.turn)
                pe.wait_ge(C.gather[st.b], 16 * st.turn)
            pe.wait_ge(B.copied, G)

            def tick(at):
                if at(1).exists:
                    dense_transposes(C, at(1), rows, c_ready)
                if at(2).exists:
                    dense_products(C, at(2), W2s)
            ticks(pe, tick, 2)
            pe.wait_ge(C.edge, STEPS)
            pe.wait_ge(C.node, STEPS)
            scatter(D, True)
            pe.wait_ge(D.copied, G)

            def tick(at):
                st = at(2)
                if st.exists:
                    pe.wait_ge(e_lo, st.k + 1)
                    for m in range(HB):
                        c = slice(m * P, (m + 1) * P)
                        if st.after(1):
                            pe.wait_ge(e_z1, st.k * HB + (m + 1 - HB))
                        pe.matmul(bank[m][:], w1x_hi[:, c], h_hi[:], start=True, stop=False)
                        pe.matmul(bank[m][:], w1x_hi[:, c], h_lo[:], start=False, stop=False)
                        pe.matmul(bank[m][:], w1x_lo[:, c], h_hi[:], start=False, stop=False)
                        pe.matmul(bank[m][:], w1a_hi[:, c], a_parts[:], start=False, stop=False)
                        pe.matmul(bank[m][:], w1a_lo[0:FA, c], a_parts[0:FA, :], start=False, stop=True).then_inc(e_L1, 1)
                st = at(1)
                if st.exists:
                    pe.wait_ge(e_normed, st.k + 1)
                    if st.after(1):
                        pe.wait_ge(e_lo, st.k)
                    for s in range(T):
                        pe.transpose(bank[5][:, s * P:(s + 1) * P], normed[:, st.b, s, :], ident[:])
                        last = pe.transpose(bank[6][:, s * P:(s + 1) * P],
                                            node_out[:, st.b, s, F:F + P], ident[:])
                    last.then_inc(e_T, 1)
                st = at(4)
                if st.exists:
                    pe.wait_ge(e_z2, st.k * HB + HB)
                    if st.after(1):
                        pe.wait_ge(e_out, st.k)
                    for s in range(T):
                        for c in range(HB):
                            last = pe.matmul(bank[4][:, s * P:(s + 1) * P], z2[:, c, s * P:(s + 1) * P], w3s[:, c, :],
                                             start=(c == 0), stop=(c == HB - 1))
                    last.then_inc(e_L3, 1)
                st = at(3)
                if st.exists:
                    pe.wait_ge(e_z1lo, st.k * HB + HB)
                    d = st.b % 2
                    for m in range(HB):
                        cols = slice(m * P, (m + 1) * P)
                        if st.after(1):
                            pe.wait_ge(e_z2, st.k * HB + (m + 1 - HB))
                        for c in range(HB):
                            pe.matmul(bank[2 + m][:], w2_hi[:, c, cols], z1_hi[:, d, c, :], start=(c == 0), stop=False)
                            pe.matmul(bank[2 + m][:], w2_hi[:, c, cols], z1_lo[:, d, c, :], start=False, stop=False)
                            last = pe.matmul(bank[2 + m][:], w2_lo[:, c, cols], z1_hi[:, d, c, :], start=False,
                                             stop=(c == HB - 1))
                        last.then_inc(e_L2, 1)
            pe.wait_ge(s_split, 3)
            ticks(pe, tick, 4)


_INS = ['x', 'src', 'dst', 'edge_attr_64', 'L0_gnn_W1', 'L0_gnn_b1', 'L0_gnn_W2', 'L0_gnn_b2', 'L1_gnn_u',
        'L1_gnn_w1', 'L1_gnn_b1', 'L1_gnn_w2', 'L1_gnn_b2', 'L1_gnn_w3', 'L1_gnn_b3']


def kernel(**inputs):
    import numpy as _np
    import concourse.bacc as _bacc
    from concourse import mybir as _mybir
    from concourse.bass_utils import run_bass_kernel_spmd as _run

    nc = _bacc.Bacc("TRN2", target_bir_lowering=False, num_devices=1)
    arrays, args = {}, []
    for name in _INS:
        a = _np.ascontiguousarray(inputs[name])
        arrays[f"in_{name}_dram"] = a
        args.append(nc.dram_tensor(f"in_{name}_dram", a.shape, _mybir.dt.from_np(a.dtype), kind="ExternalInput").ap())
    shape = arrays["in_x_dram"].shape
    args.append(nc.dram_tensor("out_0_dram", shape, _mybir.dt.from_np(_np.dtype('float32')), kind="ExternalOutput").ap())
    gnn_kernel(nc, *args)
    r = _run(nc, [arrays], core_ids=[0])
    return r.results[0]["out_0_dram"]
```
